# Optimizing a Trainium2 kernel written in Bass

```python
import numpy as np
import jax
import jax.numpy as jnp

def _softmax(x, axis=-1):
    return jax.nn.softmax(x, axis=axis)

def _gelu(x):
    return jax.nn.gelu(x, approximate=True)

def _silu(x):
    return jax.nn.silu(x)

def _sigmoid(x):
    return jax.nn.sigmoid(x)

def _layernorm(x, axis=-1, eps=1e-05):
    m = jnp.mean(x, axis=axis, keepdims=True)
    v = jnp.var(x, axis=axis, keepdims=True)
    return (x - m) / jnp.sqrt(v + eps)

def _scatter_add(tgt, idx, src, axis=0):
    return tgt.at[idx].add(src)

def _segment_sum(src, seg, n):
    return jax.ops.segment_sum(src, seg, n)
kernel_name = 'mk_gnn_preln_d2_gnn_r32_b66fb5'

def setup_inputs(seed: int=0):
    np.random.seed(seed)
    _w = jnp.asarray

    def _rec_inputs():
        import jax
        import jax.numpy as jnp
        _gk = jax.random.key(seed)
        x = -8.776e-05 + 1 * jax.random.normal(jax.random.fold_in(_gk, 1), (625, 256), jnp.float32)
        _s = jax.random.randint(jax.random.fold_in(_gk, 2), (5000,), 0, 625, jnp.int32)
        _d = jax.random.randint(jax.random.fold_in(_gk, 3), (5000,), 0, 625, jnp.int32)
        _loop = jnp.arange(625, dtype=jnp.int32)
        src = jnp.concatenate([_s, _d, _loop])
        dst = jnp.concatenate([_d, _s, _loop])
        _o = jnp.argsort(dst, stable=True)
        src = src[_o]
        dst = dst[_o]
        edge_weight = jax.random.uniform(jax.random.fold_in(_gk, 12), (10625,), jnp.float32, 0.0, 1)
        return (x, src, dst, edge_weight)
    x, src, dst, edge_weight = _rec_inputs()

    def _L0_gnn_setup():
        import jax, jax.numpy as jnp
        import numpy as np
        N = 625
        E = 10000
        DIN = 256
        DOUT = 256
        L = 3

        def _edge_conv(x, src, dst, W, b):
            xi = x[dst]
            xj = x[src]
            m = jnp.concatenate([xi, xj - xi], axis=-1) @ W + b
            s = jax.ops.segment_sum(m, dst, num_segments=N)
            cnt = jax.ops.segment_sum(jnp.ones((dst.shape[0],), m.dtype), dst, num_segments=N)
            return s / jnp.maximum(cnt, 1.0)[:, None]
        key = jax.random.key(seed)
        ks = jax.random.split(key, 4 + 2 * L)
        x = jax.random.normal(ks[0], (N, DIN), dtype=jnp.float32)
        edge_index = jax.random.randint(ks[1], (2, E), 0, N, dtype=jnp.int64)
        scale = 0.05
        inp = {'x': x, 'edge_index': edge_index}
        din = DIN
        for l in range(L):
            inp[f'W{l}'] = jax.random.normal(ks[2 + l], (2 * din, DOUT), dtype=jnp.float32) * scale
            inp[f'b{l}'] = jnp.zeros((DOUT,), dtype=jnp.float32)
            din = DOUT
        cat_dim = DIN + L * DOUT
        inp['Wf'] = jax.random.normal(ks[2 + L], (cat_dim, DOUT), dtype=jnp.float32) * scale
        inp['bf'] = jnp.zeros((DOUT,), dtype=jnp.float32)
        return inp
    _L0_gnn_all = _L0_gnn_setup()
    _L0_gnn_in = {k: v for k, v in _L0_gnn_all.items() if k in ('W0', 'b0', 'W1', 'b1', 'W2', 'b2', 'Wf', 'bf')}
    del _L0_gnn_all

    def _L1_gnn_setup():
        import jax, jax.numpy as jnp
        import numpy as np
        N = 3125
        NNZ = 100000
        IN_DIM = 256
        OUT_DIM = 256
        BN_EPS = 1e-05
        key = jax.random.key(seed)
        ks = jax.random.split(key, 6)
        x = jax.random.normal(ks[0], (N, IN_DIM), dtype=jnp.float32)
        A_indices = jax.random.randint(ks[1], (2, NNZ), 0, N, dtype=jnp.int64)
        A_values = jax.random.uniform(ks[2], (NNZ,), dtype=jnp.float32)
        W = jax.random.normal(ks[3], (IN_DIM, OUT_DIM), dtype=jnp.float32) / np.sqrt(IN_DIM)
        bias = jax.random.normal(ks[4], (OUT_DIM,), dtype=jnp.float32) * 0.02
        gamma = jnp.ones((OUT_DIM,), dtype=jnp.float32)
        beta = jnp.zeros((OUT_DIM,), dtype=jnp.float32)
        return {'x': x, 'A_indices': A_indices, 'A_values': A_values, 'A_shape': N, 'W': W, 'bias': bias, 'gamma': gamma, 'beta': beta}
    _L1_gnn_all = _L1_gnn_setup()
    _L1_gnn_in = {k: v for k, v in _L1_gnn_all.items() if k in ('W', 'bias', 'gamma', 'beta')}
    del _L1_gnn_all
    return {'x': x, 'src': src, 'dst': dst, 'edge_weight': edge_weight, 'L0_gnn_W0': _L0_gnn_in['W0'], 'L0_gnn_b0': _L0_gnn_in['b0'], 'L0_gnn_W1': _L0_gnn_in['W1'], 'L0_gnn_b1': _L0_gnn_in['b1'], 'L0_gnn_W2': _L0_gnn_in['W2'], 'L0_gnn_b2': _L0_gnn_in['b2'], 'L0_gnn_Wf': _L0_gnn_in['Wf'], 'L0_gnn_bf': _L0_gnn_in['bf'], 'L1_gnn_W': _L1_gnn_in['W'], 'L1_gnn_bias': _L1_gnn_in['bias'], 'L1_gnn_gamma': _L1_gnn_in['gamma'], 'L1_gnn_beta': _L1_gnn_in['beta']}

def reference(x, src, dst, edge_weight, L0_gnn_W0, L0_gnn_b0, L0_gnn_W1, L0_gnn_b1, L0_gnn_W2, L0_gnn_b2, L0_gnn_Wf, L0_gnn_bf, L1_gnn_W, L1_gnn_bias, L1_gnn_gamma, L1_gnn_beta):
    import jax
    import jax.numpy as jnp

    def _L0_gnn_ref(x, edge_index, W0, b0, W1, b1, W2, b2, Wf, bf):
        import jax, jax.numpy as jnp
        import numpy as np
        N = 625
        E = 10000
        DIN = 256
        DOUT = 256
        L = 3

        def _edge_conv(x, src, dst, W, b):
            xi = x[dst]
            xj = x[src]
            m = jnp.concatenate([xi, xj - xi], axis=-1) @ W + b
            s = jax.ops.segment_sum(m, dst, num_segments=N)
            cnt = jax.ops.segment_sum(jnp.ones((dst.shape[0],), m.dtype), dst, num_segments=N)
            return s / jnp.maximum(cnt, 1.0)[:, None]
        src, dst = (edge_index[0], edge_index[1])
        xs = [x]
        h = x
        for W, b in ((W0, b0), (W1, b1), (W2, b2)):
            h = jax.nn.relu(_edge_conv(h, src, dst, W, b))
            xs.append(h)
        cat = jnp.concatenate(xs, axis=-1)
        return cat @ Wf + bf

    def _L1_gnn_ref(x, A_indices, A_values, A_shape, W, bias, gamma, beta):
        import jax, jax.numpy as jnp
        import numpy as np
        N = 3125
        NNZ = 100000
        IN_DIM = 256
        OUT_DIM = 256
        BN_EPS = 1e-05
        h = jnp.einsum('nd,df->nf', x, W)
        row, col = (A_indices[0], A_indices[1])
        gathered = A_values[:, None] * h[col]
        agg = jax.ops.segment_sum(gathered, row, num_segments=A_shape)
        h = agg + bias
        mean = jnp.mean(h, axis=0)
        var = jnp.mean(jnp.square(h - mean), axis=0)
        h = (h - mean) * jax.lax.rsqrt(var + BN_EPS) * gamma + beta
        return jax.nn.relu(h)
    edge_index = jnp.stack([src, dst])
    h = jnp.maximum(_layernorm(x, axis=-1), 0.0)
    x = x + _L0_gnn_ref(h, edge_index, L0_gnn_W0, L0_gnn_b0, L0_gnn_W1, L0_gnn_b1, L0_gnn_W2, L0_gnn_b2, L0_gnn_Wf, L0_gnn_bf)
    h = jnp.maximum(_layernorm(x, axis=-1), 0.0)
    x = x + _L1_gnn_ref(h, edge_index, edge_weight, 625, L1_gnn_W, L1_gnn_bias, L1_gnn_gamma, L1_gnn_beta)
    return x

_drawn_inputs = setup_inputs


def setup_inputs(seed=0):
    import zlib

    import numpy as np

    out = dict(_drawn_inputs(seed))
    spreads = {'L0_gnn_b0': (0.0, 0.1),
     'L0_gnn_b1': (0.0, 0.1),
     'L0_gnn_b2': (0.0, 0.1),
     'L0_gnn_bf': (0.0, 0.1),
     'L1_gnn_gamma': (1.0, 0.2),
     'L1_gnn_beta': (0.0, 0.1)}
    factors = {}
    for name, (base, spread) in spreads.items():
        noise = np.random.default_rng([zlib.crc32(name.encode()), seed]).standard_normal(out[name].shape)
        drawn = base * np.exp(spread * noise) if base else spread * noise
        out[name] = jnp.asarray(drawn.astype(out[name].dtype))
    for name, factor in factors.items():
        out[name] = (out[name] * factor).astype(out[name].dtype)
    return out
```

```python
from contextlib import ExitStack

import concourse.bass as bass
from concourse import mybir

F32 = mybir.dt.float32
F32R = mybir.dt.float32r
BF16 = mybir.dt.bfloat16
F16 = mybir.dt.float16
I32 = mybir.dt.int32
U8 = mybir.dt.uint8
ALU = mybir.AluOpType
ACT = mybir.ActivationFunctionType
AX = mybir.AxisListType

P = 128
NODES = 625
EDGES = 10625
D = 256
KF = D // P
LAYERS = 3
NB = 5
BLK = NODES // NB
EP = 125
TILES = EDGES // EP
PER = TILES // NB
NODES_E = NODES + 1
HALVES = ((0, 312), (312, NODES_E))
KINDS = 4
WINDOW = 32
MARGIN = 12
PRE = PER + 2
RING = 48
OH = (NB - 1) * BLK + P
SLOW = 5
EPS = 1e-5

assert EP * TILES == EDGES and PER * NB == TILES and BLK * NB == NODES


def window_base(t):
    c, j = divmod(t, PER)
    return BLK * c + 22 * (j // 3) + 7 * (j % 3) - MARGIN


def window_pieces(r):
    out = []
    for t in range(TILES):
        base = window_base(t)
        lo, hi = max(base, BLK * r), min(base + WINDOW, BLK * (r + 1))
        if lo < hi:
            out.append((t, lo - base, lo - BLK * r, hi - lo))
    return out


def last_block(t):
    return min((window_base(t) + WINDOW - 1) // BLK, NB - 1)


class Steps:

    def __init__(self, eng, sem):
        self.eng, self.sem, self.n = eng, sem, 0

    def add(self, ins):
        self.n += 1
        ins.then_inc(self.sem, 1)
        return self.n

    def wait(self, n=None):
        self.eng.wait_ge(self.sem, self.n if n is None else n)


class Groups:

    def __init__(self, filled, banks):
        self.filled, self.banks = filled, banks
        self.index, self.bank, self.read, self.earlier = {}, {}, {}, {}
        self.last = {b: None for b in range(len(banks))}

    def plan(self, names, banks, read, first):
        for i, name in enumerate(names):
            b = banks[len(self.index) % len(banks)]
            self.index[name] = len(self.index)
            self.bank[name], self.read[name] = self.banks[b], (read, first + i)
            self.earlier[name], self.last[b] = self.last[b], name

    def wait_free(self, eng, name):
        if self.earlier[name] is not None:
            eng.wait_ge(*self.read[self.earlier[name]])

    def wait_filled(self, eng, name):
        eng.wait_ge(self.filled, self.index[name] + 1)


def gnn_kernel(nc, x, src, dst, edge_weight, W0, b0, W1, b1, W2, b2, Wf, bf, W4, b4, gamma, beta, out):
    with ExitStack() as ctx:
        def psum(name, shape, dt):
            return ctx.enter_context(nc.psum_tensor(name, shape, dt))

        def sem(name):
            return ctx.enter_context(nc.semaphore(name))

        arena_base = (nc.sbuf_base + 31) // 32 * 32
        arena_top = [0]

        def size(shape, dt):
            n = 1
            for s in shape[1:]:
                n *= s
            return (n * {F32: 4, F32R: 4, I32: 4, BF16: 2, F16: 2}[dt] + 31) // 32 * 32

        def sb(name, shape, dt):
            t = nc.alloc_sbuf_tensor_at(name, shape, dt, offset=arena_base + arena_top[0])
            arena_top[0] += size(shape, dt)
            return t

        def overlay(start, end, specs):
            made = []
            for name, shape, dt in specs:
                made.append(nc.alloc_sbuf_tensor_at(name, shape, dt, offset=arena_base + start))
                start += size(shape, dt)
            assert start <= end, (start, end)
            return made

        ident = sb("ident", [P, P], F32)
        ones_r = sb("ones_r", [BLK, P], F32R)
        ones_f = sb("ones_f", [BLK, P], F32)
        node_id = sb("node_id", [EP, OH], F16)
        zeros_bf = sb("zeros_bf", [EP, P], BF16)
        base_id = sb("base_id", [EP, NB, 18], F32)
        flag = sb("flag", [1, 1], I32)
        edge_rows_i = sb("edge_rows_i", [TILES, 2, EP], I32)
        edge_rows = sb("edge_rows", [TILES, 3, EP], F32)
        edge_cols = sb("edge_cols", [EP, 3, TILES], F32)
        weight_rest = sb("weight_rest", [EP, 2, TILES], F32)
        weight_parts = sb("weight_parts", [EP, 3, TILES], BF16)
        parts_f = sb("parts_f", [EP, 3, TILES], F32)
        rel = sb("rel", [EP, NB, PER], F32)
        dev = sb("dev", [EP, TILES], F32)
        dev_max = sb("dev_max", [EP, 1], F32)
        worst = sb("worst", [1, 1], F32)
        counts = sb("counts", [BLK, NB, NODES_E], F32R)
        weights = sb("weights", [BLK, NB, NODES], F32)
        low = sb("low", [BLK, 5, BLK], F32)
        x_in = sb("x_in", [BLK, NB, D], F32)
        bf_all = sb("bf_all", [BLK, D], F32)
        vec_rows = sb("vec_rows", [6 * KF, P], F32)
        vecs = sb("vecs", [P, 6 * KF], F32)
        stats = sb("stats", [P, NB, 6], F32)
        moments = sb("moments", [P, NB, 2], F32)
        rstd = sb("rstd", [P, NB], F32)
        shift = sb("shift", [P, NB], F32)
        h0_hi = sb("h0_hi", [P, KF, NODES_E], F32R)
        h0_lo = sb("h0_lo", [P, KF, NODES_E], F32R)
        RAW = 4
        raw = [sb(f"raw{i}", [P, 2 * KF, D], F32) for i in range(RAW)]
        wd = [[sb(f"wd{l}_{s}", [P, KF, D], F32R) for s in ("hi", "lo")] for l in range(LAYERS)]
        wb = [[sb(f"wb{l}_{s}", [P, KF, D], F32R) for s in ("hi", "lo")] for l in range(LAYERS)]
        wf = [sb(f"wf_{s}", [P, 4 * KF, D], F32R) for s in ("hi", "lo")]
        w4 = [sb(f"w4_{s}", [P, KF, D], F32R) for s in ("hi", "lo")]

        spare0 = arena_top[0]
        arena_top[0] += size([P, NB, NODES_E], F32R)
        (h0,) = overlay(spare0, arena_top[0], [("h0", [BLK, NB, D], F32)])
        (counts_lo,) = overlay(spare0, arena_top[0], [("counts_lo", [BLK, NB, NODES_E], F32R)])
        h4_hi, h4_lo = overlay(spare0, arena_top[0], [("h4_hi", [P, KF, NODES], F32R),
                                                      ("h4_lo", [P, KF, NODES], F32R)])
        build0 = arena_top[0]
        src_hot = sb("src_hot", [EP, RING, OH], BF16)
        dst_hot = sb("dst_hot", [EP, TILES, KINDS, WINDOW], BF16)
        build1 = arena_top[0]
        (h1_hi, h1_lo, h2_hi, h2_lo, h3_hi, h3_lo, u_hi, u_lo, weights_hi, weights_lo,
         inv_count, has_edge, own, pre) = overlay(build0, build1, [
             ("h1_hi", [P, KF, NODES_E], F32R), ("h1_lo", [P, KF, NODES_E], F32R),
             ("h2_hi", [P, KF, NODES_E], F32R), ("h2_lo", [P, KF, NODES_E], F32R),
             ("h3_hi", [P, KF, NODES_E], F32R), ("h3_lo", [P, KF, NODES_E], F32R),
             ("u_hi", [BLK, NB, D], F32R), ("u_lo", [BLK, NB, D], F32R),
             ("weights_hi", [BLK, NB, NODES_E], F32R), ("weights_lo", [BLK, NB, NODES_E], F32R),
             ("inv_count", [P, NODES_E], F32), ("has_edge", [P, NODES_E], F32),
             ("own", [P, KF, NODES_E], F32), ("pre", [P, 1280], F32)])
        h_hi, h_lo = [h0_hi, h1_hi, h2_hi, h3_hi], [h0_lo, h1_lo, h2_lo, h3_lo]
        pre_t = pre[:, 0:KF * NODES_E].rearrange("p (f n) -> p f n", f=KF)
        h4_rows = pre[0:BLK, 0:NB * D].rearrange("p (b d) -> p b d", b=NB)
        fence = ctx.enter_context(nc.sbuf_tensor("arena", [P, arena_top[0] + 32], U8))

        bank = [psum(f"bank{i}", [P, 512], F32) for i in range(8)]
        built = [bank[i][:, :].rearrange("p (k n) -> p k n", k=KINDS) for i in range(NB)]

        edges_loaded = sem("edges_loaded")
        vecs_loaded = sem("vecs_loaded")
        x_loaded = sem("x_loaded")
        bias_loaded = sem("bias_loaded")
        raw_loaded = [sem(f"raw_loaded{i}") for i in range(RAW)]
        constants_ready = sem("constants_ready")
        pool_steps = sem("pool_steps")
        vector_steps = sem("vector_steps")
        scalar_steps = sem("scalar_steps")
        edge_rows_ready = sem("edge_rows_ready")
        edge_cols_ready = sem("edge_cols_ready")
        window_ready = sem("window_ready")
        parts_ready = sem("parts_ready")
        dev_ready = sem("dev_ready")
        flag_ready = sem("flag_ready")
        src_hot_ready = sem("src_hot_ready")
        slow_slot_ready = sem("slow_slot_ready")
        slow_slot_free = sem("slow_slot_free")
        high_window_ready = sem("high_window_ready")
        low_window_ready = sem("low_window_ready")
        block_built = sem("block_built")
        block_copied = sem("block_copied")
        block_low = sem("block_low")
        weights_summed = sem("weights_summed")
        variance_ready = sem("variance_ready")
        std_ready = sem("std_ready")
        norm_ready = sem("norm_ready")
        h0_ready = sem("h0_ready")
        w_diff = sem("w_diff")
        w_hi = sem("w_hi")
        w_lo = sem("w_lo")
        filled = sem("filled")
        h0_lo_ready = sem("h0_lo_ready")
        h_hi_ready = sem("h_hi_ready")
        h_lo_ready = sem("h_lo_ready")
        u_hi_ready = sem("u_hi_ready")
        u_lo_ready = sem("u_lo_ready")
        own_ready = sem("own_ready")
        own_masked = sem("own_masked")
        inv_ready = sem("inv_ready")
        z_filled = sem("z_filled")
        z_drained = sem("z_drained")
        z_ready = sem("z_ready")
        weights_t_hi = sem("weights_t_hi")
        weights_t_lo = sem("weights_t_lo")
        vecs_ready = sem("vecs_ready")
        xb_ready = sem("xb_ready")
        x1_ready = sem("x1_ready")
        norm4_ready = sem("norm4_ready")
        h4_rows_ready = sem("h4_rows_ready")
        h4_hi_ready = sem("h4_hi_ready")
        h4_lo_ready = sem("h4_lo_ready")
        agg_ready = sem("agg_ready")
        bn_ready = sem("bn_ready")
        y_ready = sem("y_ready")
        out_ready = sem("out_ready")
        out_stored = sem("out_stored")

        groups = Groups(filled, bank)
        early, spare = (5, 6, 7), (4, 5, 6, 7)
        groups.plan(["edges"], early, edge_cols_ready, 1)
        groups.plan(["vecs"], early, vecs_ready, 1)
        groups.plan(["dev"], early, flag_ready, 1)
        groups.plan([("h0", b) for b in range(NB)], early, h0_lo_ready, 1)
        for l in range(LAYERS):
            groups.plan([("u", l, b) for b in range(NB)], spare, u_lo_ready, NB * l + 1)
            groups.plan([("own", l, q) for q in range(4)], spare, own_ready, 4 * l + 1)
            if l == 0:
                groups.plan([("cnt", h) for h in range(2)], spare, inv_ready, 1)
            if l == 1:
                groups.plan([("wt", i) for i in range(NB + 2)], spare, weights_t_lo, 1)
        groups.plan([("head", b) for b in range(NB)], spare, x1_ready, 1)
        groups.plan([("h4", b) for b in range(NB)], spare, h4_lo_ready, 1)
        groups.plan([("g", b) for b in range(NB)], spare, u_lo_ready, NB * LAYERS + 1)
        groups.plan([("y", b) for b in range(NB)], spare, out_ready, 1)

        QUADS = [(f, h) for h in range(2) for f in range(KF)]

        rows = lambda w: w.rearrange("(c p) n -> p c n", p=P)
        raw_plan = [(0, rows(W0)), (1, rows(W1)), (2, rows(W2)), (3, rows(Wf)[:, 0:4, :]),
                    (0, rows(Wf)[:, 4:8, :]), (1, rows(W4))]

        block = ctx.enter_context(nc.Block())

        @block.sync
        def _(sp):
            sp.dma_start(edge_rows_i[:, 0, :], src.rearrange("(t p) -> t p", p=EP)).then_inc(edges_loaded, 16)
            sp.dma_start(edge_rows_i[:, 1, :], dst.rearrange("(t p) -> t p", p=EP)).then_inc(edges_loaded, 16)
            sp.dma_start(edge_rows[:, 2, :], edge_weight.rearrange("(t p) -> t p", p=EP)).then_inc(edges_loaded, 16)
            sp.dma_start(x_in[:, :, :], x.rearrange("(b p) d -> p b d", p=BLK)).then_inc(x_loaded, 16)
            for i, v in enumerate((b0, b1, b2, b4, gamma, beta)):
                sp.dma_start(vec_rows[KF * i:KF * i + KF, :], v.rearrange("(f p) -> f p", p=P)).then_inc(vecs_loaded, 16)
            for i, (slot, source) in enumerate(raw_plan):
                if i >= RAW:
                    sp.wait_ge(w_lo, 2 * (slot + 1))
                sp.dma_start(raw[slot][:, 0:source.shape[1], :], source).then_inc(raw_loaded[slot], 16)
            sp.dma_start(bf_all[:, :], bf.rearrange("(a d) -> a d", a=1).broadcast_to([BLK, D])).then_inc(bias_loaded, 16)
            for b in range(NB):
                sp.wait_ge(out_ready, b + 1)
                sp.dma_start(out[BLK * b:BLK * b + BLK, :], x_in[:, b, :]).then_inc(out_stored, 16)
            sp.wait_ge(out_stored, 16 * NB)

        @block.gpsimd
        def _(pool):
            step = Steps(pool, pool_steps)
            step.add(pool.memset(ident[:, :], 0.0))
            step.wait()
            pool.affine_select(out=ident[:, :], in_=ident[:, :], compare_op=ALU.not_equal, fill=1.0,
                               base=0, pattern=[[-1, P]], channel_multiplier=1).then_inc(constants_ready, 1)
            pool.iota(base_id[:, :, :].rearrange("p c (a b) -> p c a b", b=3),
                      [[BLK, NB], [22, 6], [7, 3]], base=-MARGIN, channel_multiplier=0,
                      allow_small_or_imprecise_dtypes=True).then_inc(constants_ready, 1)
            pool.iota(node_id[:, :], [[1, OH]], base=0, channel_multiplier=0,
                      allow_small_or_imprecise_dtypes=True).then_inc(constants_ready, 1)
            pool.memset(ones_f[:, :], 1.0)
            pool.memset(zeros_bf[:, :], 0.0)
            pool.memset(counts[:, :, NODES:NODES_E].bitcast(F32), 0.0)
            pool.memset(h0_hi[:, :, NODES:NODES_E].bitcast(F32), 0.0)
            pool.memset(h0_lo[:, :, NODES:NODES_E].bitcast(F32), 0.0).then_inc(constants_ready, 1)

            for c in range(NB):
                pool.wait_ge(window_ready, c + 1)
                pool.wait_ge(parts_ready, 1)
                hot = dst_hot[:, PER * c:PER * (c + 1), :, :]
                for k in (2, 3):
                    part = weight_parts[:, k - 1, PER * c:PER * (c + 1)].unsqueeze(2).to_broadcast([EP, PER, WINDOW])
                    ins = pool.tensor_tensor(hot[:, :, k, :], hot[:, :, 0, :], part, ALU.mult)
                ins.then_inc(low_window_ready, 1)

            def difference(l):
                r = raw[l]
                pool.wait_ge(raw_loaded[l], 16)
                pool.tensor_tensor(r[:, 0:KF, :], r[:, 0:KF, :], r[:, KF:2 * KF, :], ALU.subtract).then_inc(w_diff, 1)

            def split_layer(l):
                r = raw[l]
                pool.wait_ge(w_hi, 2 * l + 2)
                pool.tensor_tensor(wd[l][1][:, :, :], r[:, 0:KF, :], wd[l][0][:, :, :].bitcast(F32),
                                   ALU.subtract).then_inc(w_lo, 1)
                pool.tensor_tensor(wb[l][1][:, :, :], r[:, KF:2 * KF, :], wb[l][0][:, :, :].bitcast(F32),
                                   ALU.subtract).then_inc(w_lo, 1)

            def split_rest(i, hi, lo, r):
                pool.wait_ge(w_hi, 2 * LAYERS + i + 1)
                pool.tensor_tensor(lo, r, hi.bitcast(F32), ALU.subtract).then_inc(w_lo, 1)

            def sum_weights(g):
                r, s = divmod(g, NB)
                pool.wait_ge(block_copied, g + 1)
                pool.wait_ge(block_low, g + 1)
                w = weights[:, s, BLK * r:BLK * (r + 1)]
                pool.tensor_tensor(w, w, low[:, g % 5, :], ALU.add).then_inc(weights_summed, 1)

            for l in range(LAYERS):
                difference(l)
            split_layer(0)
            for g in range(NB * NB):
                sum_weights(g)
                if g == 4:
                    split_layer(1)
                if g == 9:
                    split_layer(2)
                if g == 14:
                    split_rest(0, wf[0][:, 0:4, :], wf[1][:, 0:4, :], raw[3][:, :, :])
                if g == 19:
                    split_rest(1, wf[0][:, 4:8, :], wf[1][:, 4:8, :], raw[0][:, :, :])
                    split_rest(2, w4[0][:, :, :], w4[1][:, :, :], raw[1][:, 0:KF, :])
            pool.wait_ge(block_built, NB * NB)
            for t in (weights_hi, weights_lo):
                pool.memset(t[:, :, NODES:NODES_E].bitcast(F32), 0.0)
            pool.wait_ge(bias_loaded, 16)
            pool.wait_ge(h0_ready, NB)
            pool.wait_ge(norm_ready, 1)
            pool.tensor_tensor(x_in[:, :, :], x_in[:, :, :],
                               bf_all[:, :].unsqueeze(1).to_broadcast([BLK, NB, D]), ALU.add).then_inc(xb_ready, 1)
            for l in range(LAYERS):
                for q, (f, h) in enumerate(QUADS):
                    a, e = HALVES[h]
                    if l == 0:
                        pool.wait_ge(inv_ready, h + 1)
                    pool.wait_ge(own_ready, 4 * l + q + 1)
                    pool.tensor_tensor(own[:, f, a:e], own[:, f, a:e], has_edge[:, a:e],
                                       ALU.mult).then_inc(own_masked, 1)

        @block.vector
        def _(dve):
            step = Steps(dve, vector_steps)
            dve.wait_ge(edges_loaded, 48)
            dve.tensor_copy(edge_rows[:, 0:2, :], edge_rows_i[:, :, :]).then_inc(edge_rows_ready, 1)
            dve.wait_ge(x_loaded, 16)

            def moments_of(b, source):
                n = step.add(dve.bn_stats(stats[0:BLK, b, :], source))
                step.wait(n)
                step.add(dve.bn_aggr(moments[0:BLK, b, :], stats[0:BLK, b, :]))

            stds = [0]

            def inverse_std(o, variance):
                stds[0] += 1
                dve.tensor_scalar(o, variance, EPS, None, ALU.add).then_inc(variance_ready, 1)
                dve.wait_ge(std_ready, stds[0])
                step.add(dve.reciprocal(o, o))
                step.wait()

            def scale_shift(b0_, b1_, ready):
                step.wait()
                inverse_std(rstd[0:BLK, b0_:b1_], moments[0:BLK, b0_:b1_, 1])
                dve.scalar_tensor_tensor(out=shift[0:BLK, b0_:b1_], in0=moments[0:BLK, b0_:b1_, 0], scalar=-1.0,
                                         in1=rstd[0:BLK, b0_:b1_], op0=ALU.mult, op1=ALU.mult).then_inc(ready, 1)

            dve.wait_ge(constants_ready, 4)
            step.add(dve.tensor_copy(ones_r[:, :], ones_f[:, :]))
            groups.wait_filled(dve, "edges")
            e3 = groups.bank["edges"][0:EP, 0:3 * TILES].rearrange("p (v t) -> p v t", v=3)
            dve.tensor_copy(edge_cols[:, :, :], e3).then_inc(edge_cols_ready, 1)
            dve.wait_ge(edge_cols_ready, 1)
            step.add(dve.tensor_tensor(rel[:, :, :], edge_cols[:, 1, :].rearrange("p (c j) -> p c j", c=NB),
                                       base_id[:, :, 0:PER], ALU.subtract))
            step.wait()
            step.add(dve.tensor_scalar(dev[:, :], rel[:, :, :].rearrange("p c j -> p (c j)"),
                                       (WINDOW - 1) / 2, None, ALU.subtract))
            w = edge_cols[:, 2, :]
            a = step.add(dve.tensor_copy(weight_parts[:, 0, :], w))
            step.wait(a)
            dve.tensor_reduce(dev_max[:, :], dev[:, :], AX.X, ALU.max, apply_absolute_value=True).then_inc(dev_ready, 1)
            step.add(dve.tensor_tensor(weight_rest[:, 0, :], w, weight_parts[:, 0, :], ALU.subtract))
            step.wait()
            step.add(dve.tensor_copy(weight_parts[:, 1, :], weight_rest[:, 0, :]))
            step.wait()
            step.add(dve.tensor_tensor(weight_rest[:, 1, :], weight_rest[:, 0, :], weight_parts[:, 1, :], ALU.subtract))
            step.wait()
            dve.tensor_copy(weight_parts[:, 2, :], weight_rest[:, 1, :]).then_inc(parts_ready, 1)
            dve.wait_ge(parts_ready, 1)
            step.add(dve.tensor_copy(parts_f[:, :, :], weight_parts[:, :, :]))

            def plain_window(c):
                hot = dst_hot[:, PER * c:PER * (c + 1), :, :]
                ids = node_id[:, 0:WINDOW].unsqueeze(1).to_broadcast([EP, PER, WINDOW])
                at = rel[:, c, :].unsqueeze(2).to_broadcast([EP, PER, WINDOW])
                dve.tensor_tensor(hot[:, :, 0, :], ids, at, ALU.is_equal).then_inc(window_ready, 1)

            def high_window(c):
                hot = dst_hot[:, PER * c:PER * (c + 1), :, :]
                dve.wait_ge(window_ready, c + 1)
                part = weight_parts[:, 0, PER * c:PER * (c + 1)].unsqueeze(2).to_broadcast([EP, PER, WINDOW])
                dve.tensor_tensor(hot[:, :, 1, :], hot[:, :, 0, :], part, ALU.mult).then_inc(high_window_ready, 1)

            def source_tile(t):
                return dve.tensor_scalar(src_hot[:, t % RING, :], node_id[:, :], edge_cols[:, 0, t:t + 1], None,
                                         ALU.is_equal)

            plain_window(0)
            for c in range(1, NB):
                plain_window(c)
                high_window(c - 1)
            high_window(NB - 1)
            groups.wait_filled(dve, "dev")
            step.add(dve.tensor_reduce(worst[:, :], groups.bank["dev"][0:1, 0:EP], AX.X, ALU.max))
            step.wait()
            dve.tensor_scalar(flag[:, :], worst[:, :], WINDOW / 2, None, ALU.is_gt).then_inc(flag_ready, 1)
            for b in range(NB):
                moments_of(b, x_in[:, b, :])
            scale_shift(0, NB, norm_ready)
            for t in range(PRE):
                source_tile(t).then_inc(src_hot_ready, 1)
            groups.wait_filled(dve, "vecs")
            dve.tensor_copy(vecs[:, :], groups.bank["vecs"][:, 0:6 * KF]).then_inc(vecs_ready, 1)
            for b in range(NB):
                dve.wait_ge(h_hi_ready, b + 1)
                t2 = groups.bank[("h0", b)][:, 0:KF * BLK].rearrange("p (f n) -> p f n", f=KF)
                dst_cols = slice(BLK * b, BLK * (b + 1))
                dve.tensor_tensor(h0_lo[:, :, dst_cols], t2, h0_hi[:, :, dst_cols].bitcast(F32),
                                  ALU.subtract).then_inc(h0_lo_ready, 1)

            def add_low(g):
                if g >= 5:
                    dve.wait_ge(weights_summed, g - 4)
                pair = built[g % NB][0:BLK, 2:4, 0:BLK]
                dve.tensor_reduce(low[:, g % 5, :], pair.rearrange("p k n -> p n k"), AX.X, ALU.add).then_inc(block_low, 1)

            dve.wait_ge(flag_ready, 1)
            general = dve.value_load(flag[0:1, 0:1], min_val=0, max_val=1)
            with dve.If(general > 0):
                for r in range(NB):
                    with dve.Fori(0, PER) as j:
                        for i in range(SLOW):
                            t = j * SLOW + i
                            dve.wait_ge(slow_slot_free, t + (TILES * r + 1))
                            dve.tensor_scalar(src_hot[:, i, :], node_id[:, :], edge_cols[:, 0, bass.ds(t, 1)], None,
                                              ALU.is_equal)
                            hot = src_hot[:, 2 * PER + i, 0:KINDS * BLK].rearrange("p (k n) -> p k n", k=KINDS)
                            ids = node_id[:, BLK * r:BLK * (r + 1)]
                            at = edge_cols[:, 1, bass.ds(t, 1)]
                            dve.tensor_scalar(hot[:, 0, :], ids, at, None, ALU.is_equal)
                            for k in range(3):
                                ins = dve.tensor_scalar(hot[:, k + 1, :], ids, at, parts_f[:, k, bass.ds(t, 1)],
                                                        ALU.is_equal, ALU.mult)
                            ins.then_inc(slow_slot_ready, 1)
                    for s in range(NB):
                        g = NB * r + s
                        dve.wait_ge(block_copied, g + 1)
                        at = slice(BLK * r, BLK * (r + 1))
                        dve.tensor_tensor(counts_lo[:, s, at], built[s][0:BLK, 0, 0:BLK],
                                          counts[:, s, at].bitcast(F32), ALU.subtract)
                        add_low(g)
                dve.memset(counts_lo[:, :, NODES:NODES_E].bitcast(F32), 0.0)
            with dve.Else():
                lows = 0
                for t in range(PRE, TILES):
                    if t >= RING:
                        done = NB * (last_block(t - RING) + 1)
                        for g in range(lows, done):
                            dve.wait_ge(block_copied, g + 1)
                            add_low(g)
                        lows = max(lows, done)
                    source_tile(t).then_inc(src_hot_ready, 1)
                for g in range(lows, NB * NB):
                    dve.wait_ge(block_copied, g + 1)
                    add_low(g)

            def low_rows(name, b, hi_ready, n, ready):
                dve.wait_ge(hi_ready, n)
                dve.tensor_tensor(u_lo[:, b, :], groups.bank[name][0:BLK, 0:D], u_hi[:, b, :].bitcast(F32),
                                  ALU.subtract).then_inc(ready, 1)

            def transposed_low(i):
                p, d_ = weights_turn(i)
                dve.wait_ge(weights_t_hi, i + 1)
                dve.tensor_tensor(d_(weights_lo), p, d_(weights_hi).bitcast(F32),
                                  ALU.subtract).then_inc(weights_t_lo, 1)

            def weights_turn(i):
                b = groups.bank[("wt", i)]
                if i < NB:
                    return b[0:BLK, 0:4 * BLK], lambda t: t[:, i, 0:4 * BLK]
                if i == NB:
                    return (b[0:BLK, 0:4 * BLK].rearrange("p (r n) -> p r n", r=4),
                            lambda t: t[:, 0:4, 4 * BLK:NODES])
                return b[0:BLK, 0:BLK], lambda t: t[:, 4, 4 * BLK:NODES]

            for l in range(LAYERS):
                if l >= 1:
                    dve.wait_ge(z_filled, 4 * l)
                for b in range(NB):
                    low_rows(("u", l, b), b, u_hi_ready, NB * l + b + 1, u_lo_ready)
                if l == 0:
                    for h, (a, e) in enumerate(HALVES):
                        groups.wait_filled(dve, ("cnt", h))
                        c = groups.bank[("cnt", h)][:, 0:e - a]
                        step.add(dve.tensor_scalar(inv_count[:, a:e], c, 1.0, None, ALU.max))
                        step.add(dve.tensor_scalar(has_edge[:, a:e], c, 1.0, None, ALU.min))
                        step.wait()
                        dve.reciprocal(inv_count[:, a:e], inv_count[:, a:e]).then_inc(inv_ready, 1)
                    dve.wait_ge(inv_ready, 2)
                if l == 1:
                    for i in range(NB + 2):
                        transposed_low(i)
                for q, (f, h) in enumerate(QUADS):
                    a, e = HALVES[h]
                    n = 4 * l + q + 1
                    dve.wait_ge(z_filled, n)
                    dve.wait_ge(h_hi_ready, NB + n - 4) if n > 4 else None
                    dve.tensor_tensor(pre_t[:, f, a:e], bank[q][:, 0:e - a], inv_count[:, a:e],
                                      ALU.mult).then_inc(z_drained, 1)
                    dve.wait_ge(z_drained, n)
                    dve.wait_ge(own_masked, n)
                    dve.tensor_tensor(pre_t[:, f, a:e], pre_t[:, f, a:e], own[:, f, a:e], ALU.add).then_inc(z_ready, 1)
                    dve.wait_ge(h_hi_ready, NB + n)
                    dve.scalar_tensor_tensor(out=h_lo[l + 1][:, f, a:e], in0=pre_t[:, f, a:e], scalar=0.0,
                                             in1=h_hi[l + 1][:, f, a:e].bitcast(F32), op0=ALU.max,
                                             op1=ALU.subtract).then_inc(h_lo_ready, 1)

            dve.wait_ge(xb_ready, 1)
            dve.wait_ge(h_lo_ready, 4 * LAYERS)
            for b in range(NB):
                groups.wait_filled(dve, ("head", b))
                dve.tensor_tensor(x_in[:, b, :], x_in[:, b, :], groups.bank[("head", b)][0:BLK, 0:D],
                                  ALU.add).then_inc(x1_ready, 1)
                dve.wait_ge(x1_ready, b + 1)
                moments_of(b, x_in[:, b, :])
                scale_shift(b, b + 1, norm4_ready)
            for b in range(NB):
                dve.wait_ge(h4_hi_ready, b + 1)
                t2 = groups.bank[("h4", b)][:, 0:KF * BLK].rearrange("p (f n) -> p f n", f=KF)
                cols = slice(BLK * b, BLK * (b + 1))
                dve.tensor_tensor(h4_lo[:, :, cols], t2, h4_hi[:, :, cols].bitcast(F32),
                                  ALU.subtract).then_inc(h4_lo_ready, 1)
            for b in range(NB):
                low_rows(("g", b), b, u_hi_ready, NB * LAYERS + b + 1, u_lo_ready)
            for f in range(KF):
                for h, (a, e) in enumerate(HALVES):
                    dve.wait_ge(agg_ready, 1 + QUADS.index((f, h)))
                    step.add(dve.bn_stats(stats[:, 2 * f + h, :], own[:, f, a:min(e, NODES)]))
                step.wait()
                step.add(dve.bn_aggr(moments[:, f, :], stats[:, 2 * f:2 * f + 2, :].rearrange("p a b -> p (a b)")))
                step.wait()
                inverse_std(rstd[:, f:f + 1], moments[:, f, 1:2])
                step.add(dve.tensor_tensor(rstd[:, f:f + 1], rstd[:, f:f + 1], vecs[:, 4 * KF + f:4 * KF + f + 1], ALU.mult))
                step.wait()
                step.add(dve.tensor_tensor(shift[:, f:f + 1], moments[:, f, 0:1], rstd[:, f:f + 1], ALU.mult))
                step.wait()
                dve.tensor_tensor(shift[:, f:f + 1], vecs[:, 5 * KF + f:5 * KF + f + 1], shift[:, f:f + 1],
                                  ALU.subtract).then_inc(bn_ready, 1)
            for b in range(NB):
                groups.wait_filled(dve, ("y", b))
                dve.tensor_tensor(x_in[:, b, :], x_in[:, b, :], groups.bank[("y", b)][0:BLK, 0:D],
                                  ALU.add).then_inc(out_ready, 1)

        @block.scalar
        def _(act):
            copy = lambda o, i: nc.scalar.activation(o, i, ACT.Copy)
            stds = [0]

            def root(o):
                stds[0] += 1
                act.wait_ge(variance_ready, stds[0])
                nc.scalar.activation(o, o, ACT.Sqrt).then_inc(std_ready, 1)

            def layer_hi(l):
                act.wait_ge(raw_loaded[l], 16)
                copy(wb[l][0][:, :, :], raw[l][:, KF:2 * KF, :]).then_inc(w_hi, 1)
                act.wait_ge(w_diff, l + 1)
                copy(wd[l][0][:, :, :], raw[l][:, 0:KF, :]).then_inc(w_hi, 1)

            root(rstd[0:BLK, 0:NB])
            act.wait_ge(norm_ready, 1)
            for b in range(NB):
                nc.scalar.activation(h0[:, b, :], x_in[:, b, :], ACT.Relu, bias=shift[0:BLK, b:b + 1],
                                     scale=rstd[0:BLK, b:b + 1]).then_inc(h0_ready, 1)
            act.wait_ge(constants_ready, 4)
            for b in range(NB):
                groups.wait_filled(act, ("h0", b))
                t2 = groups.bank[("h0", b)][:, 0:KF * BLK].rearrange("p (f n) -> p f n", f=KF)
                copy(h0_hi[:, :, BLK * b:BLK * (b + 1)], t2).then_inc(h_hi_ready, 1)
            layer_hi(0)

            def copy_block(g):
                r, s = divmod(g, NB)
                act.wait_ge(block_built, g + 1)
                cols = slice(BLK * r, BLK * (r + 1))
                copy(counts[:, s, cols], built[g % NB][0:BLK, 0, 0:BLK])
                copy(weights[:, s, cols], built[g % NB][0:BLK, 1, 0:BLK]).then_inc(block_copied, 1)

            for g in range(NB * NB):
                copy_block(g)
                if g == 2:
                    layer_hi(1)
                if g == 7:
                    layer_hi(2)
                if g == 12:
                    act.wait_ge(raw_loaded[3], 16)
                    copy(wf[0][:, 0:4, :], raw[3][:, :, :]).then_inc(w_hi, 1)
                if g == 17:
                    act.wait_ge(raw_loaded[0], 32)
                    copy(wf[0][:, 4:8, :], raw[0][:, :, :]).then_inc(w_hi, 1)
                    act.wait_ge(raw_loaded[1], 32)
                    copy(w4[0][:, :, :], raw[1][:, 0:KF, :]).then_inc(w_hi, 1)

            def high_rows(name, b, ready):
                groups.wait_filled(act, name)
                copy(u_hi[:, b, :], groups.bank[name][0:BLK, 0:D]).then_inc(ready, 1)

            def weights_turn(i):
                b = groups.bank[("wt", i)]
                if i < NB:
                    return b[0:BLK, 0:4 * BLK], weights_hi[:, i, 0:4 * BLK]
                if i == NB:
                    return (b[0:BLK, 0:4 * BLK].rearrange("p (r n) -> p r n", r=4),
                            weights_hi[:, 0:4, 4 * BLK:NODES])
                return b[0:BLK, 0:BLK], weights_hi[:, 4, 4 * BLK:NODES]

            act.wait_ge(vecs_ready, 1)
            for l in range(LAYERS):
                if l >= 1:
                    act.wait_ge(z_filled, 4 * l)
                for b in range(NB):
                    high_rows(("u", l, b), b, u_hi_ready)
                for q, (f, h) in enumerate(QUADS):
                    a, e = HALVES[h]
                    name = ("own", l, q)
                    groups.wait_filled(act, name)
                    if l >= 1:
                        act.wait_ge(z_ready, 4 * (l - 1) + q + 1)
                    nc.scalar.activation(own[:, f, a:e], groups.bank[name][:, 0:e - a], ACT.Identity,
                                         bias=vecs[:, KF * l + f:KF * l + f + 1]).then_inc(own_ready, 1)
                if l == 1:
                    for i in range(NB + 2):
                        groups.wait_filled(act, ("wt", i))
                        p, w = weights_turn(i)
                        copy(w, p).then_inc(weights_t_hi, 1)
                for q, (f, h) in enumerate(QUADS):
                    a, e = HALVES[h]
                    act.wait_ge(z_ready, 4 * l + q + 1)
                    nc.scalar.activation(h_hi[l + 1][:, f, a:e], pre_t[:, f, a:e], ACT.Relu).then_inc(h_hi_ready, 1)
            act.wait_ge(h_lo_ready, 4 * LAYERS)
            for b in range(NB):
                root(rstd[0:BLK, b:b + 1])
                act.wait_ge(norm4_ready, b + 1)
                nc.scalar.activation(h4_rows[:, b, :], x_in[:, b, :], ACT.Relu, bias=shift[0:BLK, b:b + 1],
                                     scale=rstd[0:BLK, b:b + 1]).then_inc(h4_rows_ready, 1)
            for b in range(NB):
                groups.wait_filled(act, ("h4", b))
                t2 = groups.bank[("h4", b)][:, 0:KF * BLK].rearrange("p (f n) -> p f n", f=KF)
                copy(h4_hi[:, :, BLK * b:BLK * (b + 1)], t2).then_inc(h4_hi_ready, 1)
            for b in range(NB):
                high_rows(("g", b), b, u_hi_ready)
            for q, (f, h) in enumerate(QUADS):
                a, e = HALVES[h]
                act.wait_ge(z_filled, 4 * LAYERS + q + 1)
                nc.scalar.activation(own[:, f, a:e], bank[q][:, 0:e - a], ACT.Identity,
                                     bias=vecs[:, KF * 3 + f:KF * 3 + f + 1]).then_inc(agg_ready, 1)
            act.wait_ge(h4_hi_ready, NB)
            for f in range(KF):
                root(rstd[:, f:f + 1])
                act.wait_ge(bn_ready, f + 1)
                act.wait_ge(filled, groups.index[("h4", NB - 1)] + 1)
                nc.scalar.activation(pre_t[:, f, 0:NODES], own[:, f, 0:NODES], ACT.Relu, bias=shift[:, f:f + 1],
                                     scale=rstd[:, f:f + 1]).then_inc(y_ready, 1)

        @block.tensor
        def _(pe):
            def three(o, lhs, rhs, start, stop):
                (lh, ll), (rh, rl) = lhs, rhs
                pe.matmul(o, lh, rh, start=start, stop=False)
                pe.matmul(o, ll, rh, start=False, stop=False)
                return pe.matmul(o, lh, rl, start=False, stop=stop)

            def fill(name):
                groups.wait_free(pe, name)
                return groups.bank[name]

            pe.wait_ge(constants_ready, 1)
            pe.wait_ge(edge_rows_ready, 1)
            e3 = groups.bank["edges"]
            for v in range(3):
                ins = pe.transpose(e3[0:EP, TILES * v:TILES * (v + 1)], edge_rows[:, v, :], ident[0:TILES, 0:TILES])
            ins.then_inc(filled, 1)
            pe.wait_ge(vecs_loaded, 16 * 6)
            pe.transpose(groups.bank["vecs"][:, 0:6 * KF], vec_rows[:, :], ident[0:6 * KF, 0:6 * KF]).then_inc(filled, 1)
            pe.wait_ge(dev_ready, 1)
            pe.transpose(groups.bank["dev"][0:1, 0:EP], dev_max[:, :], ident[0:EP, 0:EP]).then_inc(filled, 1)
            for b in range(NB):
                pe.wait_ge(h0_ready, b + 1)
                o = fill(("h0", b))
                for f in range(KF):
                    ins = pe.transpose(o[:, BLK * f:BLK * (f + 1)], h0[:, b, P * f:P * (f + 1)], ident[0:BLK, 0:BLK])
                ins.then_inc(filled, 1)

            pe.wait_ge(flag_ready, 1)
            general = pe.value_load(flag[0:1, 0:1], min_val=0, max_val=1)
            with pe.If(general > 0):
                pe.wait_ge(src_hot_ready, PRE)
                for i in range(SLOW):
                    pe.matmul(bank[0][:, 0:P], zeros_bf[:, :], zeros_bf[:, :], start=True, stop=True).then_inc(slow_slot_free, 1)
                for r in range(NB):
                    for s in range(NB):
                        if r:
                            pe.wait_ge(block_copied, NB * (r - 1) + s + 1)
                            pe.wait_ge(block_low, NB * (r - 1) + s + 1)
                        pe.matmul(bank[s][:, :], zeros_bf[:, :], node_id[:, 0:512], start=True, stop=False,
                                  skip_group_check=True)
                    with pe.Fori(0, PER) as j:
                        for i in range(SLOW):
                            pe.wait_ge(slow_slot_ready, j * SLOW + (TILES * r + i + 1))
                            hot = src_hot[:, 2 * PER + i, 0:KINDS * BLK].rearrange("p (k n) -> p k n", k=KINDS)
                            for s in range(NB):
                                ins = pe.matmul(built[s][:, :, 0:BLK], src_hot[:, i, BLK * s:BLK * s + P], hot,
                                                start=False, stop=False, skip_group_check=True)
                            ins.then_inc(slow_slot_free, 1)
                    for s in range(NB):
                        pe.matmul(built[s][:, :, 0:BLK], zeros_bf[:, :],
                                  node_id[:, 0:KINDS * BLK].rearrange("p (k n) -> p k n", k=KINDS),
                                  start=False, stop=True, skip_group_check=True).then_inc(block_built, 1)
            with pe.Else():
                for r in range(NB):
                    pieces = window_pieces(r)
                    for s in range(NB):
                        g = NB * r + s
                        if g >= NB:
                            pe.wait_ge(block_copied, g - NB + 1)
                            pe.wait_ge(block_low, g - NB + 1)
                        for i, (t, c0, n0, n) in enumerate(pieces):
                            if s == 0 and (i == 0 or t % PER == 0):
                                pe.wait_ge(high_window_ready, t // PER + 1)
                                pe.wait_ge(low_window_ready, t // PER + 1)
                            if s == 0:
                                pe.wait_ge(src_hot_ready, t + 1)
                            ins = pe.matmul(built[s][:, :, n0:n0 + n], src_hot[:, t % RING, BLK * s:BLK * s + P],
                                            dst_hot[:, t, :, c0:c0 + n], start=(i == 0), stop=(i == len(pieces) - 1),
                                            skip_group_check=True)
                        ins.then_inc(block_built, 1)

            for l in range(LAYERS):
                hh, hl = h_hi[l], h_lo[l]
                for b in range(NB):
                    if l == 0 and b == 0:
                        pe.wait_ge(block_low, NB * NB)
                        pe.wait_ge(block_copied, NB * NB)
                        pe.wait_ge(h0_lo_ready, NB)
                        pe.wait_ge(w_lo, 2)
                    if l >= 1 and b == 0:
                        pe.wait_ge(h_lo_ready, 4 * (l - 1) + 2)
                        pe.wait_ge(h_hi_ready, NB + 4 * (l - 1) + 2)
                        pe.wait_ge(w_lo, 2 * (l + 1))
                    if l >= 1 and b == 2:
                        pe.wait_ge(h_lo_ready, 4 * l)
                        pe.wait_ge(h_hi_ready, NB + 4 * l)
                    o = fill(("u", l, b))
                    cols = slice(BLK * b, BLK * (b + 1))
                    for k in range(KF):
                        ins = three(o[0:BLK, 0:D], (hh[:, k, cols], hl[:, k, cols]),
                                    (wb[l][0][:, k, :], wb[l][1][:, k, :]), k == 0, k == KF - 1)
                    ins.then_inc(filled, 1)
                for q, (f, h) in enumerate(QUADS):
                    a, e = HALVES[h]
                    o = fill(("own", l, q))
                    fc = slice(P * f, P * (f + 1))
                    for k in range(KF):
                        ins = three(o[:, 0:e - a], (wd[l][0][:, k, fc], wd[l][1][:, k, fc]),
                                    (hh[:, k, a:e], hl[:, k, a:e]), k == 0, k == KF - 1)
                    ins.then_inc(filled, 1)
                if l == 0:
                    for h, (a, e) in enumerate(HALVES):
                        o = fill(("cnt", h))[:, 0:e - a]
                        pe.matmul(o, ones_r[:, :], counts[:, 0, a:e], start=True, stop=False, skip_group_check=True)
                        with pe.If(general > 0):
                            for k in range(NB):
                                pe.matmul(o, ones_r[:, :], counts_lo[:, k, a:e], start=False, stop=False,
                                          skip_group_check=True)
                        for k in range(1, NB):
                            ins = pe.matmul(o, ones_r[:, :], counts[:, k, a:e], start=False, stop=(k == NB - 1),
                                            skip_group_check=True)
                        ins.then_inc(filled, 1)
                if l == 1:
                    pe.wait_ge(weights_summed, NB * NB)
                    for i in range(NB + 2):
                        o = fill(("wt", i))
                        if i < NB:
                            todo = [(i, s, s) for s in range(4)]
                        elif i == NB:
                            todo = [(r, 4, r) for r in range(4)]
                        else:
                            todo = [(4, 4, 0)]
                        for r, s, at in todo:
                            ins = pe.transpose(o[0:BLK, BLK * at:BLK * (at + 1)], weights[:, s, BLK * r:BLK * (r + 1)],
                                               ident[0:BLK, 0:BLK])
                        ins.then_inc(filled, 1)
                if l:
                    pe.wait_ge(z_drained, 4 * l)
                pe.wait_ge(u_lo_ready, NB * l + 1)
                for q, (f, h) in enumerate(QUADS):
                    a, e = HALVES[h]
                    pe.matmul(bank[q][:, 0:e - a], u_hi[:, 0, P * f:P * (f + 1)], counts[:, 0, a:e],
                              start=True, stop=False, skip_group_check=True)
                with pe.If(general > 0):
                    pe.wait_ge(u_lo_ready, NB * (l + 1))
                    for q, (f, h) in enumerate(QUADS):
                        a, e = HALVES[h]
                        for k in range(NB):
                            for u in (u_hi, u_lo):
                                pe.matmul(bank[q][:, 0:e - a], u[:, k, P * f:P * (f + 1)], counts_lo[:, k, a:e],
                                          start=False, stop=False, skip_group_check=True)
                for h in range(2):
                    a, e = HALVES[h]
                    for k in range(NB):
                        if h == 0:
                            pe.wait_ge(u_lo_ready, NB * l + k + 1)
                        for f in range(KF):
                            q = KF * h + f
                            for u in (u_hi, u_lo)[(k == 0):]:
                                ins = pe.matmul(bank[q][:, 0:e - a], u[:, k, P * f:P * (f + 1)], counts[:, k, a:e],
                                                start=False, stop=(k == NB - 1 and u is u_lo), skip_group_check=True)
                            if k == NB - 1:
                                ins.then_inc(z_filled, 1)

            pe.wait_ge(w_lo, 2 * LAYERS + 2)
            pe.wait_ge(h_lo_ready, 4 * LAYERS)
            pe.wait_ge(h_hi_ready, NB + 4 * LAYERS)
            for b in range(NB):
                o = fill(("head", b))
                cols = slice(BLK * b, BLK * (b + 1))
                for c in range(4 * KF):
                    l, k = divmod(c, KF)
                    ins = three(o[0:BLK, 0:D], (h_hi[l][:, k, cols], h_lo[l][:, k, cols]),
                                (wf[0][:, c, :], wf[1][:, c, :]), c == 0, c == 4 * KF - 1)
                ins.then_inc(filled, 1)
            for b in range(NB):
                pe.wait_ge(h4_rows_ready, b + 1)
                o = fill(("h4", b))
                for f in range(KF):
                    ins = pe.transpose(o[:, BLK * f:BLK * (f + 1)], h4_rows[:, b, P * f:P * (f + 1)], ident[0:BLK, 0:BLK])
                ins.then_inc(filled, 1)
            pe.wait_ge(w_lo, 2 * LAYERS + 3)
            for b in range(NB):
                o = fill(("g", b))
                pe.wait_ge(h4_lo_ready, b + 1)
                cols = slice(BLK * b, BLK * (b + 1))
                for k in range(KF):
                    ins = three(o[0:BLK, 0:D], (h4_hi[:, k, cols], h4_lo[:, k, cols]),
                                (w4[0][:, k, :], w4[1][:, k, :]), k == 0, k == KF - 1)
                ins.then_inc(filled, 1)
            pe.wait_ge(z_drained, 4 * LAYERS)
            pe.wait_ge(u_lo_ready, NB * (LAYERS + 1))
            for q, (f, h) in enumerate(QUADS):
                a, e = HALVES[h]
                for k in range(NB):
                    ins = three(bank[q][:, 0:e - a], (u_hi[:, k, P * f:P * (f + 1)], u_lo[:, k, P * f:P * (f + 1)]),
                                (weights_hi[:, k, a:e], weights_lo[:, k, a:e]), k == 0, k == NB - 1)
                ins.then_inc(z_filled, 1)
            for b in range(NB):
                o = fill(("y", b))
                for f in range(KF):
                    pe.wait_ge(y_ready, f + 1)
                    ins = pe.transpose(o[0:BLK, P * f:P * (f + 1)], pre_t[:, f, BLK * b:BLK * (b + 1)], ident[:, :])
                ins.then_inc(filled, 1)


_INS = ['x', 'src', 'dst', 'edge_weight', 'L0_gnn_W0', 'L0_gnn_b0', 'L0_gnn_W1', 'L0_gnn_b1', 'L0_gnn_W2', 'L0_gnn_b2',
        'L0_gnn_Wf', 'L0_gnn_bf', 'L1_gnn_W', 'L1_gnn_bias', 'L1_gnn_gamma', 'L1_gnn_beta']


def kernel(**inputs):
    import numpy as _np
    import concourse.bacc as _bacc
    from concourse.bass_utils import run_bass_kernel_spmd as _run

    nc = _bacc.Bacc("TRN2", target_bir_lowering=False, num_devices=1)
    arrays, args = {}, []
    for name in _INS:
        a = _np.ascontiguousarray(inputs[name])
        arrays[f"in_{name}_dram"] = a
        args.append(nc.dram_tensor(f"in_{name}_dram", a.shape, mybir.dt.from_np(a.dtype), kind="ExternalInput").ap())
    args.append(nc.dram_tensor("out_dram", (NODES, D), F32, kind="ExternalOutput").ap())
    gnn_kernel(nc, *args)
    return _run(nc, [arrays], core_ids=[0]).results[0]["out_dram"]
```

```python
from contextlib import ExitStack

import concourse.bass as bass
from concourse import mybir

F32 = mybir.dt.float32
F32R = mybir.dt.float32r
BF16 = mybir.dt.bfloat16
F16 = mybir.dt.float16
I32 = mybir.dt.int32
U8 = mybir.dt.uint8
ALU = mybir.AluOpType
ACT = mybir.ActivationFunctionType
AX = mybir.AxisListType

P = 128
NODES = 625
EDGES = 10625
D = 256
KF = D // P
LAYERS = 3
NB = 5
BLK = NODES // NB
EP = 125
TILES = EDGES // EP
PER = TILES // NB
NODES_E = NODES + 1
HALVES = ((0, 312), (312, NODES_E))
KINDS = 4
WINDOW = 28
MARGIN = 10
PRE = PER + 2
RING = 46
OH = (NB - 1) * BLK + P
SLOW = 5
STAGES = 5
LOW_AFTER = (33, 53, 74)
HEAD_AFTER = 46
EPS = 1e-5
SCALAR_TILES = (0, 6, 10)

assert EP * TILES == EDGES and PER * NB == TILES and BLK * NB == NODES


def window_base(t):
    c, j = divmod(t, PER)
    return BLK * c + 22 * (j // 3) + 7 * (j % 3) - MARGIN


def window_pieces(r):
    out = []
    for t in range(TILES):
        base = window_base(t)
        lo, hi = max(base, BLK * r), min(base + WINDOW, BLK * (r + 1))
        if lo < hi:
            out.append((t, lo - base, lo - BLK * r, hi - lo))
    return out


def last_block(t):
    return min((window_base(t) + WINDOW - 1) // BLK, NB - 1)


class Steps:

    def __init__(self, eng, sem):
        self.eng, self.sem, self.n = eng, sem, 0

    def add(self, ins):
        self.n += 1
        ins.then_inc(self.sem, 1)
        return self.n

    def wait(self, n=None):
        self.eng.wait_ge(self.sem, self.n if n is None else n)


class Groups:

    def __init__(self, filled, banks):
        self.filled, self.banks = filled, banks
        self.index, self.bank, self.read, self.earlier = {}, {}, {}, {}
        self.last = {b: None for b in range(len(banks))}
        self.turn = 0

    def plan(self, names, read, first, banks=None):
        for i, name in enumerate(names):
            b = banks[i] if banks and banks[i] is not None else self.spare[self.turn % len(self.spare)]
            self.turn += not banks or banks[i] is None
            self.index[name] = len(self.index)
            self.bank[name], self.read[name] = self.banks[b], (read, first + i)
            self.earlier[name], self.last[b] = self.last[b], name

    def wait_free(self, eng, name):
        if self.earlier[name] is not None:
            eng.wait_ge(*self.read[self.earlier[name]])

    def wait_filled(self, eng, name):
        eng.wait_ge(self.filled, self.index[name] + 1)


def gnn_kernel(nc, x, src, dst, edge_weight, W0, b0, W1, b1, W2, b2, Wf, bf, W4, b4, gamma, beta, out):
    with ExitStack() as ctx:
        def psum(name, shape, dt):
            return ctx.enter_context(nc.psum_tensor(name, shape, dt))

        def sem(name):
            return ctx.enter_context(nc.semaphore(name))

        arena_base = (nc.sbuf_base + 31) // 32 * 32
        arena_top = [0]

        def size(shape, dt):
            n = 1
            for s in shape[1:]:
                n *= s
            return (n * {F32: 4, F32R: 4, I32: 4, BF16: 2, F16: 2}[dt] + 31) // 32 * 32

        def sb(name, shape, dt):
            t = nc.alloc_sbuf_tensor_at(name, shape, dt, offset=arena_base + arena_top[0])
            arena_top[0] += size(shape, dt)
            return t

        def overlay(start, end, specs):
            made = []
            for name, shape, dt in specs:
                made.append(nc.alloc_sbuf_tensor_at(name, shape, dt, offset=arena_base + start))
                start += size(shape, dt)
            assert start <= end, (start, end)
            return made

        ident = sb("ident", [P, P], F32)
        ones_r = sb("ones_r", [BLK, 2], F32R)
        ones_f = sb("ones_f", [BLK, 2], F32)
        node_id = sb("node_id", [EP, OH], F16)
        zeros_bf = sb("zeros_bf", [EP, P], BF16)
        base_id = sb("base_id", [EP, NB, 18], F32)
        flag = sb("flag", [1, 1], I32)
        eps = sb("eps", [P, 1], F32)
        root_table = sb("root_table", [1, 1], F32)
        edge_rows_i = sb("edge_rows_i", [TILES, 2, EP], I32)
        edge_rows = sb("edge_rows", [TILES, 3, EP], F32)
        edge_cols = sb("edge_cols", [EP, 3, TILES], F32)
        weight_rest = sb("weight_rest", [EP, 2, TILES], F32)
        weight_parts = sb("weight_parts", [EP, 3, TILES], BF16)
        parts_f = sb("parts_f", [EP, 3, TILES], F32)
        rel = sb("rel", [EP, NB, PER], F32)
        dev = sb("dev", [EP, TILES], F32)
        dev_max = sb("dev_max", [EP, 1], F32)
        worst = sb("worst", [1, 1], F32)
        distance = sb("distance", [EP, OH], F16)
        counts = sb("counts", [BLK, NB, NODES_E], F32R)
        weights = sb("weights", [BLK, NB, NODES], F32)
        stage = sb("stage", [BLK, STAGES, KINDS - 1, BLK], F32)
        count_cols = sb("count_cols", [BLK, 2, NB], F32)
        x_in = sb("x_in", [BLK, NB, D], F32)
        bf_all = sb("bf_all", [BLK, D], F32)
        vec_rows = sb("vec_rows", [6 * KF, P], F32)
        vecs = sb("vecs", [P, 6 * KF], F32)
        stats = sb("stats", [P, NB, 6], F32)
        moments = sb("moments", [P, NB, 2], F32)
        rstd = sb("rstd", [P, NB], F32)
        shift = sb("shift", [P, NB], F32)
        h0_hi = sb("h0_hi", [P, KF, NODES_E], F32R)
        h0_lo = sb("h0_lo", [P, KF, NODES_E], F32R)
        u_hi = sb("u_hi", [BLK, NB, D], F32R)
        u_lo = sb("u_lo", [BLK, NB, D], F32R)
        own = sb("own", [P, KF, NODES_E], F32)
        RAW = 3
        raw = [sb(f"raw{i}", [P, 2 * KF, D], F32) for i in range(RAW)]
        wd = [[sb(f"wd{l}_{s}", [P, KF, D], F32R) for s in ("hi", "lo")] for l in range(LAYERS)]
        wb = [[sb(f"wb{l}_{s}", [P, KF, D], F32R) for s in ("hi", "lo")] for l in range(LAYERS)]
        wf01 = [sb(f"wf01_{s}", [P, 2 * KF, D], F32R) for s in ("hi", "lo")]

        spare0 = arena_top[0]
        arena_top[0] += size([P, NB, NODES_E], F32R)
        (h0,) = overlay(spare0, arena_top[0], [("h0", [BLK, NB, D], F32)])
        (counts_lo,) = overlay(spare0, arena_top[0], [("counts_lo", [BLK, NB, NODES_E], F32R)])
        h4_hi, h4_lo = overlay(spare0, arena_top[0], [("h4_hi", [P, KF, NODES], F32R),
                                                      ("h4_lo", [P, KF, NODES], F32R)])
        build0 = arena_top[0]
        src_hot = sb("src_hot", [EP, RING, OH], BF16)
        dst_hot = sb("dst_hot", [EP, TILES, KINDS, WINDOW], BF16)
        build1 = arena_top[0]
        (h1_hi, h1_lo, h2_hi, h2_lo, h3_hi, h3_lo, weights_hi, weights_lo, wf23_hi, wf23_lo, inv_count, has_edge,
         pre) = overlay(build0, build1, [
             ("h1_hi", [P, KF, NODES_E], F32R), ("h1_lo", [P, KF, NODES_E], F32R),
             ("h2_hi", [P, KF, NODES_E], F32R), ("h2_lo", [P, KF, NODES_E], F32R),
             ("h3_hi", [P, KF, NODES_E], F32R), ("h3_lo", [P, KF, NODES_E], F32R),
             ("weights_hi", [BLK, NB, NODES_E], F32R), ("weights_lo", [BLK, NB, NODES_E], F32R),
             ("wf23_hi", [P, 2 * KF, D], F32R), ("wf23_lo", [P, 2 * KF, D], F32R),
             ("inv_count", [P, NODES_E], F32), ("has_edge", [P, NODES_E], F32),
             ("pre", [P, 1280], F32)])
        w4 = wb[0]
        wf_of = lambda l, s: ((wf01[s], KF * l) if l < 2 else ((wf23_hi, wf23_lo)[s], KF * (l - 2)))
        h_hi, h_lo = [h0_hi, h1_hi, h2_hi, h3_hi], [h0_lo, h1_lo, h2_lo, h3_lo]
        pre_t = pre[:, 0:KF * NODES_E].rearrange("p (f n) -> p f n", f=KF)
        h4_rows = pre[0:BLK, 0:NB * D].rearrange("p (b d) -> p b d", b=NB)
        fence = ctx.enter_context(nc.sbuf_tensor("arena", [P, arena_top[0] + 32], U8))

        bank = [psum(f"bank{i}", [P, 512], F32) for i in range(8)]
        built = [bank[i][:, :].rearrange("p (k n) -> p k n", k=KINDS) for i in range(NB)]

        edges_loaded = sem("edges_loaded")
        edge_weights_loaded = sem("edge_weights_loaded")
        vecs_loaded = sem("vecs_loaded")
        x_loaded = sem("x_loaded")
        bias_loaded = sem("bias_loaded")
        raw_loaded = [sem(f"raw_loaded{i}") for i in range(RAW)]
        ident_ready = sem("ident_ready")
        constants_ready = sem("constants_ready")
        pool_steps = sem("pool_steps")
        vector_steps = sem("vector_steps")
        edge_rows_ready = sem("edge_rows_ready")
        edge_cols_ready = sem("edge_cols_ready")
        parts_ready = sem("parts_ready")
        window_ready = sem("window_ready")
        high_window_ready = sem("high_window_ready")
        weighted_windows_ready = sem("weighted_windows_ready")
        dev_ready = sem("dev_ready")
        flag_ready = sem("flag_ready")
        src_hot_vector = sem("src_hot_vector")
        src_hot_scalar = sem("src_hot_scalar")
        distance_ready = sem("distance_ready")
        slow_slot_ready = sem("slow_slot_ready")
        slow_slot_free = sem("slow_slot_free")
        block_built = sem("block_built")
        block_copied = sem("block_copied")
        block_rest = sem("block_rest")
        weights_summed = sem("weights_summed")
        variance_ready = sem("variance_ready")
        std_ready = sem("std_ready")
        norm_ready = sem("norm_ready")
        h0_ready = sem("h0_ready")
        h0_lo_ready = sem("h0_lo_ready")
        w_diff = sem("w_diff")
        w_hi = sem("w_hi")
        w_lo_pool = sem("w_lo_pool")
        w_lo_vector = sem("w_lo_vector")
        filled = sem("filled")
        h_hi_ready = sem("h_hi_ready")
        h_lo_ready = sem("h_lo_ready")
        u_hi_ready = sem("u_hi_ready")
        u_lo_ready = sem("u_lo_ready")
        own_ready = sem("own_ready")
        own_masked = sem("own_masked")
        count_cols_ready = sem("count_cols_ready")
        count_rows_ready = sem("count_rows_ready")
        z_read = sem("z_read")
        z_ready = sem("z_ready")
        weights_t_hi = sem("weights_t_hi")
        weights_t_lo = sem("weights_t_lo")
        vecs_ready = sem("vecs_ready")
        xb_ready = sem("xb_ready")
        x1_added = sem("x1_added")
        norm4_ready = sem("norm4_ready")
        h4_rows_ready = sem("h4_rows_ready")
        h4_hi_ready = sem("h4_hi_ready")
        h4_lo_ready = sem("h4_lo_ready")
        bn_ready = sem("bn_ready")
        y_ready = sem("y_ready")
        out_ready = sem("out_ready")
        out_stored = sem("out_stored")

        QUADS = [(f, h) for h in range(2) for f in range(KF)]
        AGG = [(f, h) for f in range(KF) for h in range(2)]
        ROWS = ((0, 4), (4, 5))
        TURNS = [[(r, s) for s in range(4)] for r in range(NB)] + [[(r, 4) for r in range(4)], [(4, 4)]]
        WT_EARLY = 4
        Y_GROUPS = [[(0, b) for b in range(4)], [(0, 4)], [(1, 0), (1, 1)], [(1, 2), (1, 3), (1, 4)]]

        groups = Groups(filled, bank)
        groups.spare = (5, 6, 7)
        groups.plan(["edges"], edge_cols_ready, 1)
        groups.plan(["dev"], flag_ready, 1)
        groups.plan(["vecs"], vecs_ready, 1)
        groups.plan([("h0", b) for b in range(NB)], h0_lo_ready, 1)
        groups.plan([("u", 0, b) for b in range(NB)], u_lo_ready, 1)
        groups.plan([("own", 0, q) for q in range(4)], own_ready, 1)
        groups.plan([("head", 0, b) for b in range(NB)], x1_added, 1)
        groups.plan([("cnt", 0)], count_cols_ready, 1)
        groups.plan([("row", k, 0) for k in range(2)], count_rows_ready, 1)
        groups.spare, groups.turn = (4, 5, 6, 7), 0
        groups.plan([("z", 0, 0), ("z", 0, 1)], z_read, 1, banks=(0, 1))
        groups.plan([("cnt", 1)], count_cols_ready, 2)
        groups.plan([("wt", 0)], weights_t_lo, 1)
        groups.plan([("row", k, 1) for k in range(2)], count_rows_ready, 3)
        groups.plan([("z", 0, 2), ("z", 0, 3)], z_read, 3, banks=(2, 3))
        for l in range(1, LAYERS):
            groups.plan([("u", l, b) for b in range(2)], u_lo_ready, NB * l + 1)
            if l == 1:
                groups.plan([("wt", i) for i in range(1, WT_EARLY)], weights_t_lo, 2, banks=(0, 1, None, None, None, None))
            groups.plan([("u", l, b) for b in range(2, NB)], u_lo_ready, NB * l + 3)
            groups.plan([("own", l, q) for q in range(4)], own_ready, 4 * l + 1)
            groups.plan([("z", l, q) for q in range(4)], z_read, 4 * l + 1, banks=range(4))
            groups.plan([("head", l, b) for b in range(NB)], x1_added, NB * l + 1, banks=(0, 1, None, None, None))
        groups.plan([("head", LAYERS, b) for b in range(NB)], x1_added, NB * LAYERS + 1)
        groups.plan([("wt", WT_EARLY)], weights_t_lo, WT_EARLY + 1)
        groups.plan([("h4", b) for b in range(3)], h4_lo_ready, 1, banks=(0, 1, 2))
        groups.plan([("wt", i) for i in range(WT_EARLY + 1, len(TURNS))], weights_t_lo, WT_EARLY + 2)
        groups.plan([("h4", b) for b in (3, 4)], h4_lo_ready, 4, banks=(3, None))
        groups.plan([("g", b) for b in range(NB)], u_lo_ready, NB * LAYERS + 1)
        groups.plan([("agg", q) for q in range(4)], y_ready, 1, banks=range(4))
        groups.plan([("y", i) for i in range(len(Y_GROUPS))], out_ready, 1)

        rows = lambda w: w.rearrange("(c p) n -> p c n", p=P)
        raw_plan = [(0, rows(W0), None), (1, rows(W1), None), (2, rows(W2), None),
                    (0, rows(Wf)[:, 0:4, :], (w_lo_pool, 2)), (1, rows(Wf)[:, 4:8, :], (w_lo_vector, 3)),
                    (2, rows(W4), (w_lo_vector, 5))]
        LO_WB0, LO_WD0, LO_WF23, LO_W4 = [(w_lo_pool, n) for n in (1, 2, 3, 4)]
        LO_WF0, LO_W1, LO_W2, LO_WF1 = [(w_lo_vector, n) for n in (1, 3, 5, 6)]

        block = ctx.enter_context(nc.Block())

        @block.sync
        def _(sp):
            sp.dma_start(edge_rows_i[:, 0, :], src.rearrange("(t p) -> t p", p=EP)).then_inc(edges_loaded, 16)
            sp.dma_start(edge_rows_i[:, 1, :], dst.rearrange("(t p) -> t p", p=EP)).then_inc(edges_loaded, 16)
            for i, (slot, source, freed) in enumerate(raw_plan):
                if freed:
                    sp.wait_ge(*freed)
                sp.dma_start(raw[slot][:, 0:source.shape[1], :], source).then_inc(raw_loaded[slot], 16)
                if i == 0:
                    for k, v in enumerate((b0, b1, b2, b4, gamma, beta)):
                        sp.dma_start(vec_rows[KF * k:KF * k + KF, :],
                                     v.rearrange("(f p) -> f p", p=P)).then_inc(vecs_loaded, 16)
                    sp.dma_start(bf_all[:, :], bf.rearrange("(a d) -> a d", a=1).broadcast_to([BLK, D])).then_inc(bias_loaded, 16)
            for i, pairs in enumerate(Y_GROUPS):
                f, b = pairs[0]
                n = len(pairs)
                sp.wait_ge(out_ready, i + 1)
                sp.dma_start(out[BLK * b:BLK * (b + n), P * f:P * (f + 1)].rearrange("(b p) d -> p b d", p=BLK),
                             x_in[:, b:b + n, P * f:P * (f + 1)]).then_inc(out_stored, 16)
            sp.wait_ge(out_stored, 16 * len(Y_GROUPS))

        @block.gpsimd
        def _(pool):
            step = Steps(pool, pool_steps)
            step.add(pool.memset(ident[:, :], 0.0))
            step.wait()
            pool.affine_select(out=ident[:, :], in_=ident[:, :], compare_op=ALU.not_equal, fill=1.0,
                               base=0, pattern=[[-1, P]], channel_multiplier=1).then_inc(ident_ready, 1)
            pool.iota(base_id[:, :, :].rearrange("p c (a b) -> p c a b", b=3),
                      [[BLK, NB], [22, 6], [7, 3]], base=-MARGIN, channel_multiplier=0,
                      allow_small_or_imprecise_dtypes=True).then_inc(constants_ready, 1)
            pool.iota(node_id[:, :], [[1, OH]], base=0, channel_multiplier=0,
                      allow_small_or_imprecise_dtypes=True).then_inc(constants_ready, 1)
            pool.memset(eps[:, :], EPS)
            pool.memset(ones_f[:, :], 1.0)
            pool.memset(zeros_bf[:, :], 0.0)
            pool.memset(counts[:, :, NODES:NODES_E].bitcast(F32), 0.0)
            pool.memset(h0_hi[:, :, NODES:NODES_E].bitcast(F32), 0.0)
            pool.memset(h0_lo[:, :, NODES:NODES_E].bitcast(F32), 0.0).then_inc(constants_ready, 1)

            pool.wait_ge(edge_cols_ready, 1)
            w = edge_cols[:, 2, :]
            for k in range(3):
                step.add(pool.tensor_copy(weight_parts[:, k, :], w))
                step.wait()
                if k < 2:
                    step.add(pool.tensor_tensor(weight_rest[:, k, :], w, weight_parts[:, k, :], ALU.subtract))
                    step.wait()
                    w = weight_rest[:, k, :]

            def weighted_windows(c, first=1):
                pool.wait_ge(window_ready, c + 1)
                hot = dst_hot[:, PER * c:PER * (c + 1), :, :]
                for k in range(first, KINDS):
                    part = weight_parts[:, k - 1, PER * c:PER * (c + 1)].unsqueeze(2).to_broadcast([EP, PER, WINDOW])
                    ins = pool.tensor_tensor(hot[:, :, k, :], hot[:, :, 0, :], part, ALU.mult)
                ins.then_inc(weighted_windows_ready, 1)

            def difference(l):
                r = raw[l]
                pool.wait_ge(raw_loaded[l], 16)
                pool.tensor_tensor(r[:, 0:KF, :], r[:, 0:KF, :], r[:, KF:2 * KF, :], ALU.subtract).then_inc(w_diff, 1)

            def low_part(n_hi, lo, source, hi):
                pool.wait_ge(w_hi, n_hi)
                pool.tensor_tensor(lo, source, hi.bitcast(F32), ALU.subtract).then_inc(w_lo_pool, 1)

            def sum_weights(g):
                r, s = divmod(g, NB)
                pool.wait_ge(block_copied, g + 1)
                part = stage[:, g % STAGES, :, :]
                step.add(pool.tensor_tensor(part[:, 1, :], part[:, 1, :], part[:, 2, :], ALU.add))
                step.wait()
                pool.tensor_tensor(weights[:, s, BLK * r:BLK * (r + 1)], part[:, 0, :], part[:, 1, :],
                                   ALU.add).then_inc(weights_summed, 1)

            weighted_windows(0, first=2)
            low_part(1, wb[0][1][:, :, :], raw[0][:, KF:2 * KF, :], wb[0][0][:, :, :])
            difference(0)
            weighted_windows(1)
            pool.wait_ge(bias_loaded, 16)
            pool.wait_ge(h0_ready, NB)
            pool.wait_ge(norm_ready, 1)
            pool.tensor_tensor(x_in[:, :, :], x_in[:, :, :],
                               bf_all[:, :].unsqueeze(1).to_broadcast([BLK, NB, D]), ALU.add).then_inc(xb_ready, 1)
            low_part(2, wd[0][1][:, :, :], raw[0][:, 0:KF, :], wd[0][0][:, :, :])
            weighted_windows(2)
            difference(1)
            difference(2)
            for g in range(NB * NB):
                sum_weights(g)
                if g == 4:
                    weighted_windows(3)
                if g == 9:
                    weighted_windows(4)
            pool.wait_ge(block_built, NB * NB)
            for t in (weights_hi, weights_lo):
                pool.memset(t[:, :, NODES:NODES_E].bitcast(F32), 0.0)
            pool.memset(inv_count[:, NODES:NODES_E], 0.0)
            pool.memset(has_edge[:, NODES:NODES_E], 0.0).then_inc(constants_ready, 1)
            pool.wait_ge(constants_ready, 4)
            for l in range(LAYERS):
                for q, (f, h) in enumerate(QUADS):
                    a, e = HALVES[h]
                    if l == 0 and f == 0:
                        pool.wait_ge(count_rows_ready, 2 if h == 0 else 4)
                    pool.wait_ge(own_ready, 4 * l + q + 1)
                    pool.tensor_tensor(own[:, f, a:e], own[:, f, a:e], has_edge[:, a:e],
                                       ALU.mult).then_inc(own_masked, 1)
                if l == 0:
                    low_part(9, wf23_lo[:, :, :], raw[1][:, :, :], wf23_hi[:, :, :])
                    low_part(10, w4[1][:, :, :], raw[2][:, 0:KF, :], w4[0][:, :, :])

        @block.vector
        def _(dve):
            step = Steps(dve, vector_steps)
            dve.wait_ge(edges_loaded, 32)
            dve.tensor_copy(edge_rows[:, 0:2, :], edge_rows_i[:, :, :]).then_inc(edge_rows_ready, 1)
            stds = [0]

            def moments_of(b):
                step.add(dve.bn_stats(stats[0:BLK, b, :], x_in[:, b, :]))

            def scale_shift(blocks, ready):
                for b in blocks:
                    step.wait(step.n - len(blocks) + 1 if b == blocks[0] else None)
                    last = dve.bn_aggr(moments[0:BLK, b, :], stats[0:BLK, b, :])
                last.then_inc(variance_ready, 1)
                stds[0] += 1
                dve.wait_ge(std_ready, stds[0])
                lo, hi = blocks[0], blocks[-1] + 1
                step.add(dve.reciprocal(rstd[0:BLK, lo:hi], rstd[0:BLK, lo:hi]))
                step.wait()
                dve.scalar_tensor_tensor(out=shift[0:BLK, lo:hi], in0=moments[0:BLK, lo:hi, 0], scalar=-1.0,
                                         in1=rstd[0:BLK, lo:hi], op0=ALU.mult, op1=ALU.mult).then_inc(ready, 1)

            groups.wait_filled(dve, "edges")
            e3 = groups.bank["edges"][0:EP, 0:3 * TILES].rearrange("p (v t) -> p v t", v=3)
            dve.tensor_copy(edge_cols[:, :, :], e3).then_inc(edge_cols_ready, 1)
            dve.wait_ge(edge_cols_ready, 1)
            dve.wait_ge(constants_ready, 1)
            step.add(dve.tensor_tensor(rel[:, :, :], edge_cols[:, 1, :].rearrange("p (c j) -> p c j", c=NB),
                                       base_id[:, :, 0:PER], ALU.subtract))
            step.wait()
            dve.wait_ge(constants_ready, 3)

            def plain_window(c):
                hot = dst_hot[:, PER * c:PER * (c + 1), :, :]
                ids = node_id[:, 0:WINDOW].unsqueeze(1).to_broadcast([EP, PER, WINDOW])
                at = rel[:, c, :].unsqueeze(2).to_broadcast([EP, PER, WINDOW])
                dve.tensor_tensor(hot[:, :, 0, :], ids, at, ALU.is_equal).then_inc(window_ready, 1)

            def high_window(c):
                hot = dst_hot[:, PER * c:PER * (c + 1), :, :]
                dve.wait_ge(pool_steps, 2)
                dve.wait_ge(window_ready, c + 1)
                part = weight_parts[:, 0, PER * c:PER * (c + 1)].unsqueeze(2).to_broadcast([EP, PER, WINDOW])
                dve.tensor_tensor(hot[:, :, 1, :], hot[:, :, 0, :], part, ALU.mult).then_inc(high_window_ready, 1)

            def source_tile(t):
                if t not in SCALAR_TILES:
                    dve.tensor_scalar(src_hot[:, t % RING, :], node_id[:, :], edge_cols[:, 0, t:t + 1], None,
                                      ALU.is_equal).then_inc(src_hot_vector, 1)

            step.add(dve.tensor_scalar(dev[:, :], rel[:, :, :].rearrange("p c j -> p (c j)"),
                                       (WINDOW - 1) / 2, None, ALU.subtract))
            plain_window(0)
            step.wait()
            dve.tensor_reduce(dev_max[:, :], dev[:, :], AX.X, ALU.max, apply_absolute_value=True).then_inc(dev_ready, 1)
            step.add(dve.tensor_copy(ones_r[:, :], ones_f[:, :]))
            dve.wait_ge(x_loaded, 16)
            for b in range(NB):
                moments_of(b)
            scale_shift(range(NB), norm_ready)
            groups.wait_filled(dve, "dev")
            step.add(dve.tensor_reduce(worst[:, :], groups.bank["dev"][0:1, 0:EP], AX.X, ALU.max))
            step.wait()
            dve.tensor_scalar(flag[:, :], worst[:, :], WINDOW / 2, None, ALU.is_gt).then_inc(flag_ready, 1)
            high_window(0)
            source_tile(1)
            source_tile(2)
            plain_window(1)
            groups.wait_filled(dve, "vecs")
            dve.tensor_copy(vecs[:, :], groups.bank["vecs"][:, 0:6 * KF]).then_inc(vecs_ready, 1)
            source_tile(3)

            def low_rows(name, b, n):
                dve.wait_ge(u_hi_ready, n)
                dve.tensor_tensor(u_lo[:, b, :], groups.bank[name][0:BLK, 0:D], u_hi[:, b, :].bitcast(F32),
                                  ALU.subtract).then_inc(u_lo_ready, 1)

            made = 4
            for b in range(NB):
                dve.wait_ge(h_hi_ready, b + 1)
                t2 = groups.bank[("h0", b)][:, 0:KF * BLK].rearrange("p (f n) -> p f n", f=KF)
                cols = slice(BLK * b, BLK * (b + 1))
                dve.tensor_tensor(h0_lo[:, :, cols], t2, h0_hi[:, :, cols].bitcast(F32),
                                  ALU.subtract).then_inc(h0_lo_ready, 1)
                source_tile(made)
                made += 1
            plain_window(2)
            for b in range(NB):
                for t in range(made, made + 2):
                    source_tile(t)
                made += 2
                low_rows(("u", 0, b), b, b + 1)
            assert made == PRE
            plain_window(3)
            plain_window(4)

            def low_part(n_hi, lo, source, hi):
                dve.wait_ge(w_hi, n_hi)
                dve.tensor_tensor(lo, source, hi.bitcast(F32), ALU.subtract).then_inc(w_lo_vector, 1)

            def low_parts(i):
                if i == 0:
                    low_part(3, wf01[1][:, 0:KF, :], raw[0][:, 0:KF, :], wf01[0][:, 0:KF, :])
                if i in (1, 2):
                    low_part(2 * i + 2, wb[i][1][:, :, :], raw[i][:, KF:2 * KF, :], wb[i][0][:, :, :])
                    low_part(2 * i + 3, wd[i][1][:, :, :], raw[i][:, 0:KF, :], wd[i][0][:, :, :])
                if i == 2:
                    low_part(8, wf01[1][:, KF:2 * KF, :], raw[0][:, KF:2 * KF, :], wf01[0][:, KF:2 * KF, :])

            def count_columns(i):
                lo, hi = ROWS[i]
                groups.wait_filled(dve, ("cnt", i))
                c = groups.bank[("cnt", i)][0:BLK, 0:2 * (hi - lo)].rearrange("p (r two) -> p r two", two=2)[:, :, 0]
                step.add(dve.tensor_scalar(count_cols[:, 0, lo:hi], c, 1.0, None, ALU.max))
                step.wait()
                dve.reciprocal(count_cols[:, 0, lo:hi], count_cols[:, 0, lo:hi])
                dve.tensor_scalar(count_cols[:, 1, lo:hi], c, 1.0, None, ALU.min).then_inc(count_cols_ready, 1)

            def add_head(l, b):
                if l == 0 and b == 0:
                    dve.wait_ge(xb_ready, 1)
                groups.wait_filled(dve, ("head", l, b))
                dve.wait_ge(x1_added, NB * (l - 1) + b + 1) if l else None
                dve.tensor_tensor(x_in[:, b, :], x_in[:, b, :], groups.bank[("head", l, b)][0:BLK, 0:D],
                                  ALU.add).then_inc(x1_added, 1)

            dve.wait_ge(flag_ready, 1)
            general = dve.value_load(flag[0:1, 0:1], min_val=0, max_val=1)
            with dve.If(general > 0):
                dve.wait_ge(pool_steps, 6)
                dve.tensor_copy(parts_f[:, :, :], weight_parts[:, :, :]).then_inc(parts_ready, 1)
                dve.wait_ge(parts_ready, 1)
                for r in range(NB):
                    with dve.Fori(0, PER) as j:
                        for i in range(SLOW):
                            t = j * SLOW + i
                            dve.wait_ge(slow_slot_free, t + (TILES * r + 1))
                            dve.tensor_scalar(src_hot[:, i, :], node_id[:, :], edge_cols[:, 0, bass.ds(t, 1)], None,
                                              ALU.is_equal)
                            hot = src_hot[:, 2 * PER + i, 0:KINDS * BLK].rearrange("p (k n) -> p k n", k=KINDS)
                            ids = node_id[:, BLK * r:BLK * (r + 1)]
                            at = edge_cols[:, 1, bass.ds(t, 1)]
                            dve.tensor_scalar(hot[:, 0, :], ids, at, None, ALU.is_equal)
                            for k in range(3):
                                ins = dve.tensor_scalar(hot[:, k + 1, :], ids, at, parts_f[:, k, bass.ds(t, 1)],
                                                        ALU.is_equal, ALU.mult)
                            ins.then_inc(slow_slot_ready, 1)
                    for s in range(NB):
                        g = NB * r + s
                        dve.wait_ge(block_copied, g + 1)
                        at = slice(BLK * r, BLK * (r + 1))
                        dve.tensor_tensor(counts_lo[:, s, at], built[s][0:BLK, 0, 0:BLK],
                                          counts[:, s, at].bitcast(F32), ALU.subtract).then_inc(block_rest, 1)
                    low_parts(r)
                    if r == 1:
                        for b in range(NB):
                            add_head(0, b)
                dve.memset(counts_lo[:, :, NODES:NODES_E].bitcast(F32), 0.0).then_inc(block_rest, 1)
            with dve.Else():
                for t in range(PRE, TILES):
                    if t >= RING:
                        dve.wait_ge(block_built, NB * (last_block(t - RING) + 1))
                    source_tile(t)
                    if t in LOW_AFTER:
                        low_parts(LOW_AFTER.index(t))
                    if HEAD_AFTER <= t < HEAD_AFTER + NB:
                        add_head(0, t - HEAD_AFTER)
            count_columns(0)

            def turned(i, t):
                b, pairs = groups.bank[("wt", i)], TURNS[i]
                r, s = pairs[0]
                if len(pairs) == 1:
                    return b[0:BLK, 0:BLK], t[:, r, BLK * s:BLK * (s + 1)]
                if pairs[1][0] == r:
                    return b[0:BLK, 0:4 * BLK], t[:, r, BLK * s:BLK * (s + 4)]
                return b[0:BLK, 0:4 * BLK].rearrange("p (r n) -> p r n", r=4), t[:, r:r + 4, BLK * s:BLK * (s + 1)]

            def z_step(l, q):
                f, h = QUADS[q]
                a, e = HALVES[h]
                n = 4 * l + q + 1
                groups.wait_filled(dve, ("z", l, q))
                if l == 0 and f == 0:
                    dve.wait_ge(count_rows_ready, 1 if h == 0 else 3)
                    dve.wait_ge(constants_ready, 4)
                dve.tensor_tensor(pre_t[:, f, a:e], groups.bank[("z", l, q)][:, 0:e - a], inv_count[:, a:e],
                                  ALU.mult).then_inc(z_read, 1)
                dve.wait_ge(z_read, n)
                dve.wait_ge(own_masked, n)
                dve.tensor_tensor(pre_t[:, f, a:e], pre_t[:, f, a:e], own[:, f, a:e], ALU.add).then_inc(z_ready, 1)

            def h_low(l, q):
                f, h = QUADS[q]
                a, e = HALVES[h]
                dve.wait_ge(h_hi_ready, NB + 4 * l + q + 1)
                dve.scalar_tensor_tensor(out=h_lo[l + 1][:, f, a:e], in0=pre_t[:, f, a:e], scalar=0.0,
                                         in1=h_hi[l + 1][:, f, a:e].bitcast(F32), op0=ALU.max,
                                         op1=ALU.subtract).then_inc(h_lo_ready, 1)

            def turned_low(i):
                dve.wait_ge(weights_t_hi, i + 1)
                p, lo = turned(i, weights_lo)
                dve.tensor_tensor(lo, p, turned(i, weights_hi)[1].bitcast(F32), ALU.subtract).then_inc(weights_t_lo, 1)

            for l in range(LAYERS):
                if l >= 1:
                    for b in range(NB):
                        if l == 1 and b == 2:
                            for i in range(1, WT_EARLY):
                                turned_low(i)
                        low_rows(("u", l, b), b, NB * l + b + 1)
                z_step(l, 0)
                if l == 0:
                    count_columns(1)
                z_step(l, 1)
                h_low(l, 0)
                h_low(l, 1)
                if l == 0:
                    turned_low(0)
                z_step(l, 2)
                z_step(l, 3)
                h_low(l, 2)
                h_low(l, 3)
                if l:
                    for b in range(NB):
                        add_head(l, b)

            for part in ((0, 1, 2), (3, 4)):
                for b in part:
                    add_head(LAYERS, b)
                for b in part:
                    dve.wait_ge(x1_added, NB * LAYERS + b + 1)
                    moments_of(b)
                scale_shift(part, norm4_ready)
            for b in range(NB):
                if b == 3:
                    turned_low(WT_EARLY)
                dve.wait_ge(h4_hi_ready, b + 1)
                t2 = groups.bank[("h4", b)][:, 0:KF * BLK].rearrange("p (f n) -> p f n", f=KF)
                cols = slice(BLK * b, BLK * (b + 1))
                dve.tensor_tensor(h4_lo[:, :, cols], t2, h4_hi[:, :, cols].bitcast(F32),
                                  ALU.subtract).then_inc(h4_lo_ready, 1)
            for i in range(WT_EARLY + 1, len(TURNS)):
                turned_low(i)
            for b in range(NB):
                low_rows(("g", b), b, NB * LAYERS + b + 1)
            vec = lambda k, f: vecs[:, KF * k + f:KF * k + f + 1]
            for f in range(KF):
                for h, (a, e) in enumerate(HALVES):
                    q = AGG.index((f, h))
                    groups.wait_filled(dve, ("agg", q))
                    step.add(dve.bn_stats(stats[:, 2 * f + h, :], groups.bank[("agg", q)][:, 0:min(e, NODES) - a]))
                step.wait()
                stds[0] += 1
                dve.bn_aggr(moments[:, f, :],
                            stats[:, 2 * f:2 * f + 2, :].rearrange("p a b -> p (a b)")).then_inc(variance_ready, 1)
                dve.wait_ge(variance_ready, stds[0])
                step.add(dve.tensor_tensor(shift[:, f:f + 1], moments[:, f, 0:1], vec(3, f), ALU.add))
                step.wait()
                step.add(dve.tensor_tensor(shift[:, f:f + 1], vec(3, f), shift[:, f:f + 1], ALU.subtract))
                dve.wait_ge(std_ready, stds[0])
                step.add(dve.reciprocal(rstd[:, f:f + 1], rstd[:, f:f + 1]))
                step.wait()
                step.add(dve.tensor_tensor(rstd[:, f:f + 1], rstd[:, f:f + 1], vec(4, f), ALU.mult))
                step.wait()
                dve.scalar_tensor_tensor(out=shift[:, f:f + 1], in0=shift[:, f:f + 1], scalar=rstd[:, f:f + 1],
                                         in1=vec(5, f), op0=ALU.mult, op1=ALU.add).then_inc(bn_ready, 1)
            for i, pairs in enumerate(Y_GROUPS):
                f, b = pairs[0]
                n = len(pairs)
                groups.wait_filled(dve, ("y", i))
                o = x_in[:, b:b + n, P * f:P * (f + 1)]
                dve.tensor_tensor(o, o, groups.bank[("y", i)][0:BLK, 0:P * n].rearrange("p (b d) -> p b d", b=n),
                                  ALU.add).then_inc(out_ready, 1)

        @block.scalar
        def _(act):
            act.dma_start(edge_rows[:, 2, :], edge_weight.rearrange("(t p) -> t p", p=EP)).then_inc(edge_weights_loaded, 16)
            act.dma_start(x_in[:, :, :], x.rearrange("(b p) d -> p b d", p=BLK)).then_inc(x_loaded, 16)
            copy = lambda o, i: nc.scalar.activation(o, i, ACT.Copy)
            stds = [0]
            act.wait_ge(ident_ready, 1)
            nc.scalar.activation(root_table[:, :], ident[0:1, 0:1], ACT.Sqrt)

            def root(o, variance):
                stds[0] += 1
                act.wait_ge(variance_ready, stds[0])
                nc.scalar.activation(o, variance, ACT.Sqrt, bias=eps[0:o.shape[0], :]).then_inc(std_ready, 1)

            def high_part(o, i):
                copy(o, i).then_inc(w_hi, 1)

            tiles_made = [0]

            def source_tile(t):
                if tiles_made[0]:
                    act.wait_ge(src_hot_scalar, tiles_made[0])
                tiles_made[0] += 1
                nc.scalar.activation(distance[:, :], node_id[:, :], ACT.Abs, bias=edge_cols[:, 0, t:t + 1],
                                     scale=-1.0).then_inc(distance_ready, 1)
                act.wait_ge(distance_ready, tiles_made[0])
                nc.scalar.activation(src_hot[:, t % RING, :], distance[:, :], ACT.Relu, bias=1.0,
                                     scale=-1.0).then_inc(src_hot_scalar, 1)

            def high_rows(name, b):
                groups.wait_filled(act, name)
                copy(u_hi[:, b, :], groups.bank[name][0:BLK, 0:D]).then_inc(u_hi_ready, 1)

            def own_terms(l, quads=range(4)):
                for q in quads:
                    f, h = QUADS[q]
                    a, e = HALVES[h]
                    groups.wait_filled(act, ("own", l, q))
                    if l >= 1:
                        act.wait_ge(z_ready, 4 * (l - 1) + q + 1)
                    nc.scalar.activation(own[:, f, a:e], groups.bank[("own", l, q)][:, 0:e - a], ACT.Identity,
                                         bias=vecs[:, KF * l + f:KF * l + f + 1]).then_inc(own_ready, 1)

            act.wait_ge(edge_cols_ready, 1)
            act.wait_ge(constants_ready, 3)
            source_tile(0)
            act.wait_ge(raw_loaded[0], 16)
            high_part(wb[0][0][:, :, :], raw[0][:, KF:2 * KF, :])
            root(rstd[0:BLK, 0:NB], moments[0:BLK, 0:NB, 1])
            act.wait_ge(norm_ready, 1)
            for b in range(NB):
                nc.scalar.activation(h0[:, b, :], x_in[:, b, :], ACT.Relu, bias=shift[0:BLK, b:b + 1],
                                     scale=rstd[0:BLK, b:b + 1]).then_inc(h0_ready, 1)
            for b in range(NB):
                if b == 3:
                    source_tile(6)
                groups.wait_filled(act, ("h0", b))
                t2 = groups.bank[("h0", b)][:, 0:KF * BLK].rearrange("p (f n) -> p f n", f=KF)
                copy(h0_hi[:, :, BLK * b:BLK * (b + 1)], t2).then_inc(h_hi_ready, 1)
            source_tile(10)
            high_rows(("u", 0, 0), 0)
            act.wait_ge(w_diff, 1)
            high_part(wd[0][0][:, :, :], raw[0][:, 0:KF, :])
            for b in range(1, NB):
                high_rows(("u", 0, b), b)
            act.wait_ge(vecs_ready, 1)

            def copy_block(g):
                r, s = divmod(g, NB)
                act.wait_ge(block_built, g + 1)
                if g >= STAGES:
                    act.wait_ge(weights_summed, g - STAGES + 1)
                copy(counts[:, s, BLK * r:BLK * (r + 1)], built[g % NB][0:BLK, 0, 0:BLK])
                copy(stage[:, g % STAGES, :, :], built[g % NB][0:BLK, 1:KINDS, 0:BLK]).then_inc(block_copied, 1)

            for r in range(NB):
                for s in range(NB):
                    copy_block(NB * r + s)
                    if r == 0 and s:
                        own_terms(0, (s - 1,))
                if r == 0:
                    act.wait_ge(raw_loaded[0], 32)
                    high_part(wf01[0][:, 0:KF, :], raw[0][:, 0:KF, :])
                    act.wait_ge(w_diff, 3)
                if r in (1, 2):
                    high_part(wb[r][0][:, :, :], raw[r][:, KF:2 * KF, :])
                    high_part(wd[r][0][:, :, :], raw[r][:, 0:KF, :])
                if r == 2:
                    high_part(wf01[0][:, KF:2 * KF, :], raw[0][:, KF:2 * KF, :])

            def count_row(k, i):
                lo, hi = ROWS[i]
                groups.wait_filled(act, ("row", k, i))
                copy((inv_count, has_edge)[k][:, BLK * lo:BLK * hi],
                     groups.bank[("row", k, i)][:, 0:BLK * (hi - lo)]).then_inc(count_rows_ready, 1)

            count_row(0, 0)
            count_row(1, 0)
            act.wait_ge(raw_loaded[1], 32)
            high_part(wf23_hi[:, :, :], raw[1][:, :, :])

            def turned(i):
                b, pairs = groups.bank[("wt", i)], TURNS[i]
                r, s = pairs[0]
                if len(pairs) == 1:
                    return b[0:BLK, 0:BLK], weights_hi[:, r, BLK * s:BLK * (s + 1)]
                if pairs[1][0] == r:
                    return b[0:BLK, 0:4 * BLK], weights_hi[:, r, BLK * s:BLK * (s + 4)]
                return (b[0:BLK, 0:4 * BLK].rearrange("p (r n) -> p r n", r=4),
                        weights_hi[:, r:r + 4, BLK * s:BLK * (s + 1)])

            def turned_high(i):
                groups.wait_filled(act, ("wt", i))
                p, hi = turned(i)
                copy(hi, p).then_inc(weights_t_hi, 1)

            for l in range(LAYERS):
                if l >= 1:
                    for b in range(NB):
                        if l == 1 and b == 2:
                            for i in range(1, WT_EARLY):
                                turned_high(i)
                        high_rows(("u", l, b), b)
                    own_terms(l)
                for q, (f, h) in enumerate(QUADS):
                    a, e = HALVES[h]
                    if l == 0 and q == 2:
                        turned_high(0)
                        count_row(0, 1)
                        count_row(1, 1)
                    act.wait_ge(z_ready, 4 * l + q + 1)
                    nc.scalar.activation(h_hi[l + 1][:, f, a:e], pre_t[:, f, a:e], ACT.Relu).then_inc(h_hi_ready, 1)
                if l == 0:
                    act.wait_ge(raw_loaded[2], 32)
                    high_part(w4[0][:, :, :], raw[2][:, 0:KF, :])
            act.wait_ge(h_lo_ready, 4 * LAYERS)
            n = 0
            for part in ((0, 1, 2), (3, 4)):
                root(rstd[0:BLK, part[0]:part[-1] + 1], moments[0:BLK, part[0]:part[-1] + 1, 1])
                n += 1
                act.wait_ge(norm4_ready, n)
                for b in part:
                    nc.scalar.activation(h4_rows[:, b, :], x_in[:, b, :], ACT.Relu, bias=shift[0:BLK, b:b + 1],
                                         scale=rstd[0:BLK, b:b + 1]).then_inc(h4_rows_ready, 1)
            for b in range(NB):
                if b == 3:
                    turned_high(WT_EARLY)
                groups.wait_filled(act, ("h4", b))
                t2 = groups.bank[("h4", b)][:, 0:KF * BLK].rearrange("p (f n) -> p f n", f=KF)
                copy(h4_hi[:, :, BLK * b:BLK * (b + 1)], t2).then_inc(h4_hi_ready, 1)
            for i in range(WT_EARLY + 1, len(TURNS)):
                turned_high(i)
            for b in range(NB):
                high_rows(("g", b), b)
            for f in range(KF):
                root(rstd[:, f:f + 1], moments[:, f, 1:2])
                act.wait_ge(bn_ready, f + 1)
                for h, (a, e) in enumerate(HALVES):
                    e = min(e, NODES)
                    q = AGG.index((f, h))
                    nc.scalar.activation(pre_t[:, f, a:e], groups.bank[("agg", q)][:, 0:e - a], ACT.Relu,
                                         bias=shift[:, f:f + 1], scale=rstd[:, f:f + 1]).then_inc(y_ready, 1)

        @block.tensor
        def _(pe):
            def three(o, lhs, rhs, start, stop):
                (lh, ll), (rh, rl) = lhs, rhs
                pe.matmul(o, lh, rh, start=start, stop=False)
                pe.matmul(o, ll, rh, start=False, stop=False)
                return pe.matmul(o, lh, rl, start=False, stop=stop)

            def fill(name):
                groups.wait_free(pe, name)
                return groups.bank[name]

            pe.wait_ge(ident_ready, 1)
            pe.wait_ge(edge_rows_ready, 1)
            pe.wait_ge(edge_weights_loaded, 16)
            e3 = fill("edges")
            for v in range(3):
                ins = pe.transpose(e3[0:EP, TILES * v:TILES * (v + 1)], edge_rows[:, v, :], ident[0:TILES, 0:TILES])
            ins.then_inc(filled, 1)
            pe.wait_ge(dev_ready, 1)
            pe.transpose(fill("dev")[0:1, 0:EP], dev_max[:, :], ident[0:EP, 0:EP]).then_inc(filled, 1)
            pe.wait_ge(vecs_loaded, 16 * 6)
            pe.transpose(fill("vecs")[:, 0:6 * KF], vec_rows[:, :], ident[0:6 * KF, 0:6 * KF]).then_inc(filled, 1)

            def turn_h0(b):
                pe.wait_ge(h0_ready, b + 1)
                o = fill(("h0", b))
                for f in range(KF):
                    ins = pe.transpose(o[:, BLK * f:BLK * (f + 1)], h0[:, b, P * f:P * (f + 1)], ident[0:BLK, 0:BLK])
                ins.then_inc(filled, 1)

            def project(name, b, lhs, rhs):
                o = fill(name)
                for k in range(len(lhs)):
                    ins = three(o[0:BLK, 0:D], lhs[k], rhs[k], k == 0, k == len(lhs) - 1)
                ins.then_inc(filled, 1)

            def feature_rows(hi, lo, b):
                return [(hi[:, k, BLK * b:BLK * (b + 1)], lo[:, k, BLK * b:BLK * (b + 1)]) for k in range(KF)]

            def neighbour_terms(l, blocks=range(NB)):
                for b in blocks:
                    if l == 0:
                        pe.wait_ge(h0_lo_ready, b + 1)
                        pe.wait_ge(*LO_WB0)
                    elif b in (0, 2):
                        pe.wait_ge(h_lo_ready, 4 * (l - 1) + (2 if b == 0 else 4))
                    project(("u", l, b), b, feature_rows(h_hi[l], h_lo[l], b),
                            [(wb[l][0][:, k, :], wb[l][1][:, k, :]) for k in range(KF)])

            def own_terms(l):
                for q, (f, h) in enumerate(QUADS):
                    a, e = HALVES[h]
                    o = fill(("own", l, q))
                    fc = slice(P * f, P * (f + 1))
                    for k in range(KF):
                        ins = three(o[:, 0:e - a], (wd[l][0][:, k, fc], wd[l][1][:, k, fc]),
                                    (h_hi[l][:, k, a:e], h_lo[l][:, k, a:e]), k == 0, k == KF - 1)
                    ins.then_inc(filled, 1)

            def head(l):
                (wh, c), (wl, _) = wf_of(l, 0), wf_of(l, 1)
                for b in range(NB):
                    if l == LAYERS and b in (0, 2):
                        pe.wait_ge(h_lo_ready, 4 * (l - 1) + (2 if b == 0 else 4))
                    project(("head", l, b), b, feature_rows(h_hi[l], h_lo[l], b),
                            [(wh[:, c + k, :], wl[:, c + k, :]) for k in range(KF)])

            def edges_into(i, r, low):
                cols = groups.bank[("cnt", i)][0:BLK, 2 * (r - ROWS[i][0]):2 * (r - ROWS[i][0]) + 2]
                parts = [counts, counts_lo] if low else [counts]
                pe.wait_ge(block_copied, NB * (r + 1))
                for part in parts:
                    for s in range(NB):
                        ins = pe.matmul(cols, part[:, s, BLK * r:BLK * (r + 1)], ones_r[:, :],
                                        start=(s == 0 and part is counts), stop=(s == NB - 1 and part is parts[-1]),
                                        skip_group_check=True)
                return ins

            def count_rows(i):
                pe.wait_ge(count_cols_ready, i + 1)
                lo, hi = ROWS[i]
                for k in range(2):
                    o = fill(("row", k, i))
                    for b in range(lo, hi):
                        ins = pe.matmul(o[:, BLK * (b - lo):BLK * (b - lo + 1)],
                                        count_cols[:, k, b:b + 1].to_broadcast([BLK, P]), ident[0:BLK, 0:BLK],
                                        start=True, stop=True)
                    ins.then_inc(filled, 1)

            def first_counts(low):
                fill(("cnt", 0))
                for r in range(*ROWS[0]):
                    ins = edges_into(0, r, low)
                ins.then_inc(filled, 1)

            turn_h0(0)
            turn_h0(1)
            turn_h0(2)
            jobs = {4: lambda: turn_h0(3), 5: lambda: turn_h0(4), 7: lambda: neighbour_terms(0, (0,)),
                    9: lambda: neighbour_terms(0, (1,)), 11: lambda: neighbour_terms(0, (2,)),
                    13: lambda: neighbour_terms(0, (3,)), 15: lambda: neighbour_terms(0, (4,))}

            def between(r):
                if r == 0:
                    pe.wait_ge(*LO_WD0)
                    own_terms(0)
                if r == 1:
                    pe.wait_ge(*LO_WF0)
                    head(0)

            pe.wait_ge(flag_ready, 1)
            general = pe.value_load(flag[0:1, 0:1], min_val=0, max_val=1)
            with pe.If(general > 0):
                for job in jobs.values():
                    job()
                pe.wait_ge(src_hot_vector, PRE - len(SCALAR_TILES))
                pe.wait_ge(src_hot_scalar, len(SCALAR_TILES))
                for i in range(SLOW):
                    pe.matmul(bank[0][:, 0:P], zeros_bf[:, :], zeros_bf[:, :], start=True, stop=True).then_inc(slow_slot_free, 1)
                for r in range(NB):
                    for s in range(NB):
                        if r:
                            pe.wait_ge(block_rest, NB * (r - 1) + s + 1)
                        pe.matmul(bank[s][:, :], zeros_bf[:, :], node_id[:, 0:512], start=True, stop=False,
                                  skip_group_check=True)
                    with pe.Fori(0, PER) as j:
                        for i in range(SLOW):
                            pe.wait_ge(slow_slot_ready, j * SLOW + (TILES * r + i + 1))
                            hot = src_hot[:, 2 * PER + i, 0:KINDS * BLK].rearrange("p (k n) -> p k n", k=KINDS)
                            for s in range(NB):
                                ins = pe.matmul(built[s][:, :, 0:BLK], src_hot[:, i, BLK * s:BLK * s + P], hot,
                                                start=False, stop=False, skip_group_check=True)
                            ins.then_inc(slow_slot_free, 1)
                    for s in range(NB):
                        pe.matmul(built[s][:, :, 0:BLK], zeros_bf[:, :],
                                  node_id[:, 0:KINDS * BLK].rearrange("p (k n) -> p k n", k=KINDS),
                                  start=False, stop=True, skip_group_check=True).then_inc(block_built, 1)
                    between(r)
                pe.wait_ge(block_rest, NB * NB + 1)
                first_counts(True)
                count_rows(0)
            with pe.Else():
                made = [0, 0]

                def wait_tile(t):
                    made[t in SCALAR_TILES] += 1
                    if t in SCALAR_TILES:
                        pe.wait_ge(src_hot_scalar, made[1])
                    else:
                        pe.wait_ge(src_hot_vector, made[0])
                    if t % PER == 0:
                        pe.wait_ge(high_window_ready, 1)
                        pe.wait_ge(weighted_windows_ready, t // PER + 1)

                seen = 0
                for r in range(NB):
                    pieces = window_pieces(r)

                    def place(s, i):
                        t, c0, n0, n = pieces[i]
                        return pe.matmul(built[s][:, :, n0:n0 + n], src_hot[:, t % RING, BLK * s:BLK * s + P],
                                         dst_hot[:, t, :, c0:c0 + n], start=(i == 0), stop=(i == len(pieces) - 1),
                                         skip_group_check=True)

                    if r <= 2:
                        for i in range(len(pieces)):
                            if r == 0 and i in jobs:
                                jobs[i]()
                            if pieces[i][0] >= seen:
                                wait_tile(seen)
                                seen += 1
                            for s in range(NB):
                                if r and i == 0:
                                    pe.wait_ge(block_copied, NB * (r - 1) + s + 1)
                                ins = place(s, i)
                                if i == len(pieces) - 1:
                                    ins.then_inc(block_built, 1)
                    else:
                        for s in range(NB):
                            pe.wait_ge(block_copied, NB * (r - 1) + s + 1)
                            for i in range(len(pieces)):
                                if pieces[i][0] >= seen:
                                    wait_tile(seen)
                                    seen += 1
                                ins = place(s, i)
                            ins.then_inc(block_built, 1)
                            if r == NB - 1 and s == 1:
                                first_counts(False)
                    between(r)
                count_rows(0)

            def sums(l, h):
                a, e = HALVES[h]
                quads = [(f, KF * h + f) for f in range(KF)]
                pe.wait_ge(u_lo_ready, NB * l + 1)
                for f, q in quads:
                    pe.matmul(fill(("z", l, q))[:, 0:e - a], u_hi[:, 0, P * f:P * (f + 1)], counts[:, 0, a:e],
                              start=True, stop=False, skip_group_check=True)
                with pe.If(general > 0):
                    pe.wait_ge(u_lo_ready, NB * (l + 1))
                    for f, q in quads:
                        for k in range(NB):
                            for u in (u_hi, u_lo):
                                pe.matmul(bank[q][:, 0:e - a], u[:, k, P * f:P * (f + 1)], counts_lo[:, k, a:e],
                                          start=False, stop=False, skip_group_check=True)
                for k in range(NB):
                    if h == 0:
                        pe.wait_ge(u_lo_ready, NB * l + k + 1)
                    for f, q in quads:
                        for u in (u_hi, u_lo)[(k == 0):]:
                            ins = pe.matmul(bank[q][:, 0:e - a], u[:, k, P * f:P * (f + 1)], counts[:, k, a:e],
                                            start=False, stop=(k == NB - 1 and u is u_lo), skip_group_check=True)
                        if k == NB - 1:
                            ins.then_inc(filled, 1)

            def turn_weights(indices):
                pe.wait_ge(weights_summed, NB * NB)
                for i in indices:
                    o = fill(("wt", i))
                    for n, (r, s) in enumerate(TURNS[i]):
                        ins = pe.transpose(o[0:BLK, BLK * n:BLK * (n + 1)], weights[:, s, BLK * r:BLK * (r + 1)],
                                           ident[0:BLK, 0:BLK])
                    ins.then_inc(filled, 1)

            for s in range(KF):
                pe.wait_ge(block_copied, NB * (NB - 1) + s + 1)
            sums(0, 0)
            fill(("cnt", 1))
            with pe.If(general > 0):
                edges_into(1, NB - 1, True).then_inc(filled, 1)
            with pe.Else():
                edges_into(1, NB - 1, False).then_inc(filled, 1)
            turn_weights((0,))
            count_rows(1)
            sums(0, 1)
            for l in range(1, LAYERS):
                pe.wait_ge(*(LO_W1 if l == 1 else LO_W2))
                neighbour_terms(l, (0, 1))
                if l == 1:
                    turn_weights(range(1, WT_EARLY))
                neighbour_terms(l, (2, 3, 4))
                own_terms(l)
                sums(l, 0)
                sums(l, 1)
                pe.wait_ge(*(LO_WF1 if l == 1 else LO_WF23))
                head(l)
            head(LAYERS)
            turn_weights((WT_EARLY,))
            for b in range(NB):
                if b == 3:
                    turn_weights(range(WT_EARLY + 1, len(TURNS)))
                pe.wait_ge(h4_rows_ready, b + 1)
                o = fill(("h4", b))
                for f in range(KF):
                    ins = pe.transpose(o[:, BLK * f:BLK * (f + 1)], h4_rows[:, b, P * f:P * (f + 1)], ident[0:BLK, 0:BLK])
                ins.then_inc(filled, 1)
            pe.wait_ge(*LO_W4)
            for b in range(NB):
                pe.wait_ge(h4_lo_ready, b + 1)
                project(("g", b), b, feature_rows(h4_hi, h4_lo, b), [(w4[0][:, k, :], w4[1][:, k, :]) for k in range(KF)])
            for q, (f, h) in enumerate(AGG):
                a, e = HALVES[h]
                o = fill(("agg", q))
                for k in range(NB):
                    if q == 0:
                        pe.wait_ge(u_lo_ready, NB * LAYERS + k + 1)
                    ins = three(o[:, 0:e - a], (u_hi[:, k, P * f:P * (f + 1)], u_lo[:, k, P * f:P * (f + 1)]),
                                (weights_hi[:, k, a:e], weights_lo[:, k, a:e]), k == 0, k == NB - 1)
                ins.then_inc(filled, 1)
            for i, pairs in enumerate(Y_GROUPS):
                o = fill(("y", i))
                for n, (f, b) in enumerate(pairs):
                    pe.wait_ge(y_ready, 2 * f + (1 if b < 2 else 2))
                    ins = pe.transpose(o[0:BLK, P * n:P * (n + 1)], pre_t[:, f, BLK * b:BLK * (b + 1)], ident[:, :])
                ins.then_inc(filled, 1)


_INS = ['x', 'src', 'dst', 'edge_weight', 'L0_gnn_W0', 'L0_gnn_b0', 'L0_gnn_W1', 'L0_gnn_b1', 'L0_gnn_W2', 'L0_gnn_b2',
        'L0_gnn_Wf', 'L0_gnn_bf', 'L1_gnn_W', 'L1_gnn_bias', 'L1_gnn_gamma', 'L1_gnn_beta']


def kernel(**inputs):
    import numpy as _np
    import concourse.bacc as _bacc
    from concourse.bass_utils import run_bass_kernel_spmd as _run

    nc = _bacc.Bacc("TRN2", target_bir_lowering=False, num_devices=1)
    arrays, args = {}, []
    for name in _INS:
        a = _np.ascontiguousarray(inputs[name])
        arrays[f"in_{name}_dram"] = a
        args.append(nc.dram_tensor(f"in_{name}_dram", a.shape, mybir.dt.from_np(a.dtype), kind="ExternalInput").ap())
    args.append(nc.dram_tensor("out_dram", (NODES, D), F32, kind="ExternalOutput").ap())
    gnn_kernel(nc, *args)
    return _run(nc, [arrays], core_ids=[0]).results[0]["out_dram"]
```

```python
from contextlib import ExitStack

import concourse.bass as bass
from concourse import mybir

F32 = mybir.dt.float32
F32R = mybir.dt.float32r
BF16 = mybir.dt.bfloat16
F16 = mybir.dt.float16
I32 = mybir.dt.int32
U8 = mybir.dt.uint8
ALU = mybir.AluOpType
ACT = mybir.ActivationFunctionType
AX = mybir.AxisListType

P = 128
NODES = 625
EDGES = 10625
D = 256
KF = D // P
LAYERS = 3
NB = 5
BLK = NODES // NB
EP = 125
TILES = EDGES // EP
PER = TILES // NB
NODES_E = NODES + 1
HALVES = ((0, 312), (312, NODES_E))
KINDS = 4
WINDOW = 28
MARGIN = 10
PRE = PER + 2
RING = 46
OH = (NB - 1) * BLK + P
SLOW = 5
STAGES = 5
LOW_AFTER = 33
HEAD_AFTER = 46
EPS = 1e-5
SCALAR_EARLY, SCALAR_LATER = (0, 6, 10), {0: (40, 43), 1: (58, 62, 66)}
SCALAR_TILES = SCALAR_EARLY + SCALAR_LATER[0] + SCALAR_LATER[1]

assert EP * TILES == EDGES and PER * NB == TILES and BLK * NB == NODES


def window_base(t):
    c, j = divmod(t, PER)
    return BLK * c + 22 * (j // 3) + 7 * (j % 3) - MARGIN


def window_pieces(r):
    out = []
    for t in range(TILES):
        base = window_base(t)
        lo, hi = max(base, BLK * r), min(base + WINDOW, BLK * (r + 1))
        if lo < hi:
            out.append((t, lo - base, lo - BLK * r, hi - lo))
    return out


def last_block(t):
    return min((window_base(t) + WINDOW - 1) // BLK, NB - 1)


class Steps:

    def __init__(self, eng, sem):
        self.eng, self.sem, self.n = eng, sem, 0

    def add(self, ins):
        self.n += 1
        ins.then_inc(self.sem, 1)
        return self.n

    def wait(self, n=None):
        self.eng.wait_ge(self.sem, self.n if n is None else n)


class Groups:

    def __init__(self, filled, banks):
        self.filled, self.banks = filled, banks
        self.index, self.bank, self.read, self.earlier = {}, {}, {}, {}
        self.last = {b: None for b in range(len(banks))}
        self.turn = 0

    def plan(self, names, read, first, banks=None):
        for i, name in enumerate(names):
            b = banks[i] if banks and banks[i] is not None else self.spare[self.turn % len(self.spare)]
            self.turn += not banks or banks[i] is None
            self.index[name] = len(self.index)
            self.bank[name], self.read[name] = self.banks[b], (read, first + i)
            self.earlier[name], self.last[b] = self.last[b], name

    def wait_free(self, eng, name):
        if self.earlier[name] is not None:
            eng.wait_ge(*self.read[self.earlier[name]])

    def wait_filled(self, eng, name):
        eng.wait_ge(self.filled, self.index[name] + 1)


def gnn_kernel(nc, x, src, dst, edge_weight, W0, b0, W1, b1, W2, b2, Wf, bf, W4, b4, gamma, beta, out):
    with ExitStack() as ctx:
        def psum(name, shape, dt):
            return ctx.enter_context(nc.psum_tensor(name, shape, dt))

        def sem(name):
            return ctx.enter_context(nc.semaphore(name))

        arena_base = (nc.sbuf_base + 31) // 32 * 32
        arena_top = [0]

        def size(shape, dt):
            n = 1
            for s in shape[1:]:
                n *= s
            return (n * {F32: 4, F32R: 4, I32: 4, BF16: 2, F16: 2}[dt] + 31) // 32 * 32

        def sb(name, shape, dt):
            t = nc.alloc_sbuf_tensor_at(name, shape, dt, offset=arena_base + arena_top[0])
            arena_top[0] += size(shape, dt)
            return t

        def overlay(start, end, specs):
            made = []
            for name, shape, dt in specs:
                made.append(nc.alloc_sbuf_tensor_at(name, shape, dt, offset=arena_base + start))
                start += size(shape, dt)
            assert start <= end, (start, end)
            return made

        ident = sb("ident", [P, P], F32)
        ones_r = sb("ones_r", [BLK, P], F32R)
        ones_f = sb("ones_f", [BLK, P], F32)
        node_id = sb("node_id", [EP, OH], F16)
        zeros_bf = sb("zeros_bf", [EP, P], BF16)
        base_id = sb("base_id", [EP, NB, 18], F32)
        flag = sb("flag", [1, 1], I32)
        eps = sb("eps", [P, 1], F32)
        root_table = sb("root_table", [1, 1], F32)
        edge_rows_i = sb("edge_rows_i", [TILES, 2, EP], I32)
        edge_rows = sb("edge_rows", [TILES, 3, EP], F32)
        edge_cols = sb("edge_cols", [EP, 3, TILES], F32)
        weight_rest = sb("weight_rest", [EP, 2, TILES], F32)
        weight_parts = sb("weight_parts", [EP, 3, TILES], BF16)
        parts_f = sb("parts_f", [EP, 3, TILES], F32)
        rel = sb("rel", [EP, NB, PER], F32)
        dev = sb("dev", [EP, TILES], F32)
        dev_max = sb("dev_max", [EP, 1], F32)
        worst = sb("worst", [1, 1], F32)
        distance = sb("distance", [EP, OH], F16)
        counts = sb("counts", [BLK, NB, NODES_E], F32R)
        weights = sb("weights", [BLK, NB, NODES], F32)
        stage = sb("stage", [BLK, STAGES, KINDS - 1, BLK], F32)
        x_in = sb("x_in", [BLK, NB, D], F32)
        bf_all = sb("bf_all", [BLK, D], F32)
        vec_rows = sb("vec_rows", [6 * KF, P], F32)
        vecs = sb("vecs", [P, 6 * KF], F32)
        stats = sb("stats", [P, NB, 6], F32)
        moments = sb("moments", [P, NB, 2], F32)
        rstd = sb("rstd", [P, NB], F32)
        scale = sb("scale", [P, KF], F32)
        shift = sb("shift", [P, NB], F32)
        h0_hi = sb("h0_hi", [P, KF, NODES_E], F32R)
        h0_lo = sb("h0_lo", [P, KF, NODES_E], F32R)
        u_hi = sb("u_hi", [BLK, NB, D], F32R)
        u_lo = sb("u_lo", [BLK, NB, D], F32R)
        own = sb("own", [P, KF, NODES_E], F32)
        RAW = 3
        raw = [sb(f"raw{i}", [P, 2 * KF, D], F32) for i in range(RAW)]
        wd = [[sb(f"wd{l}_{s}", [P, KF, D], F32R) for s in ("hi", "lo")] for l in range(LAYERS)]
        wb = [[sb(f"wb{l}_{s}", [P, KF, D], F32R) for s in ("hi", "lo")] for l in range(LAYERS)]
        wf01 = [sb(f"wf01_{s}", [P, 2 * KF, D], F32R) for s in ("hi", "lo")]

        spare0 = arena_top[0]
        arena_top[0] += size([P, NB, NODES_E], F32R)
        (h0,) = overlay(spare0, arena_top[0], [("h0", [BLK, NB, D], F32)])
        (counts_lo,) = overlay(spare0, arena_top[0], [("counts_lo", [BLK, NB, NODES_E], F32R)])
        h4_hi, h4_lo = overlay(spare0, arena_top[0], [("h4_hi", [P, KF, NODES], F32R),
                                                      ("h4_lo", [P, KF, NODES], F32R)])
        build0 = arena_top[0]
        src_hot = sb("src_hot", [EP, RING, OH], BF16)
        windows0 = arena_top[0]
        dst_hot = sb("dst_hot", [EP, TILES, KINDS, WINDOW], BF16)
        build1 = arena_top[0]
        (h1_hi, h1_lo, h2_hi, h2_lo, h3_hi, h3_lo, weights_hi, weights_lo) = overlay(build0, windows0, [
            ("h1_hi", [P, KF, NODES_E], F32R), ("h1_lo", [P, KF, NODES_E], F32R),
            ("h2_hi", [P, KF, NODES_E], F32R), ("h2_lo", [P, KF, NODES_E], F32R),
            ("h3_hi", [P, KF, NODES_E], F32R), ("h3_lo", [P, KF, NODES_E], F32R),
            ("weights_hi", [BLK, NB, NODES_E], F32R), ("weights_lo", [BLK, NB, NODES_E], F32R)])
        inv_count, has_edge = overlay(windows0, windows0 + 2 * size([EP, PER, KINDS, WINDOW], BF16), [
            ("inv_count", [P, NODES_E], F32), ("has_edge", [P, NODES_E], F32)])
        wf23_hi, wf23_lo, pre = overlay(windows0 + 2 * size([P, NODES_E], F32), build1, [
            ("wf23_hi", [P, 2 * KF, D], F32R), ("wf23_lo", [P, 2 * KF, D], F32R), ("pre", [P, 1280], F32)])
        w4 = wb[0]
        wf_of = lambda l, s: ((wf01[s], KF * l) if l < 2 else ((wf23_hi, wf23_lo)[s], KF * (l - 2)))
        h_hi, h_lo = [h0_hi, h1_hi, h2_hi, h3_hi], [h0_lo, h1_lo, h2_lo, h3_lo]
        pre_t = pre[:, 0:KF * NODES_E].rearrange("p (f n) -> p f n", f=KF)
        h4_rows = pre[0:BLK, 0:NB * D].rearrange("p (b d) -> p b d", b=NB)
        fence = ctx.enter_context(nc.sbuf_tensor("arena", [P, arena_top[0] + 32], U8))

        bank = [psum(f"bank{i}", [P, 512], F32) for i in range(8)]
        built = [bank[i][:, :].rearrange("p (k n) -> p k n", k=KINDS) for i in range(NB)]

        edges_loaded = sem("edges_loaded")
        edge_weights_loaded = sem("edge_weights_loaded")
        vecs_loaded = sem("vecs_loaded")
        x_loaded = sem("x_loaded")
        bias_loaded = sem("bias_loaded")
        raw_loaded = [sem(f"raw_loaded{i}") for i in range(RAW)]
        ident_ready = sem("ident_ready")
        ones_ready = sem("ones_ready")
        constants_ready = sem("constants_ready")
        pool_steps = sem("pool_steps")
        vector_steps = sem("vector_steps")
        edge_rows_ready = sem("edge_rows_ready")
        edge_cols_ready = sem("edge_cols_ready")
        weight_part_ready = sem("weight_part_ready")
        parts_ready = sem("parts_ready")
        window_ready = sem("window_ready")
        high_window_ready = sem("high_window_ready")
        weighted_windows_ready = sem("weighted_windows_ready")
        dev_ready = sem("dev_ready")
        flag_ready = sem("flag_ready")
        src_hot_vector = sem("src_hot_vector")
        src_hot_scalar = sem("src_hot_scalar")
        distance_ready = sem("distance_ready")
        slow_slot_ready = sem("slow_slot_ready")
        slow_slot_free = sem("slow_slot_free")
        block_built = sem("block_built")
        block_copied = sem("block_copied")
        block_rest = sem("block_rest")
        weights_summed = sem("weights_summed")
        variance_ready = sem("variance_ready")
        std_ready = sem("std_ready")
        norm_ready = sem("norm_ready")
        h0_ready = sem("h0_ready")
        h0_lo_ready = sem("h0_lo_ready")
        w_diff = sem("w_diff")
        w_hi = sem("w_hi")
        w_lo_pool = sem("w_lo_pool")
        w_lo_vector = sem("w_lo_vector")
        filled = sem("filled")
        h_hi_ready = sem("h_hi_ready")
        h_lo_ready = sem("h_lo_ready")
        u_hi_ready = sem("u_hi_ready")
        u_lo_ready = sem("u_lo_ready")
        own_ready = sem("own_ready")
        own_masked = sem("own_masked")
        has_edge_ready = sem("has_edge_ready")
        counts_bounded = sem("counts_bounded")
        count_rows_ready = sem("count_rows_ready")
        z_read = sem("z_read")
        z_ready = sem("z_ready")
        weights_t_hi = sem("weights_t_hi")
        weights_t_lo = sem("weights_t_lo")
        vecs_ready = sem("vecs_ready")
        xb_ready = sem("xb_ready")
        x1_added = sem("x1_added")
        norm4_ready = sem("norm4_ready")
        h4_rows_ready = sem("h4_rows_ready")
        h4_hi_ready = sem("h4_hi_ready")
        h4_lo_ready = sem("h4_lo_ready")
        bn_ready = sem("bn_ready")
        y_ready = sem("y_ready")
        out_ready = sem("out_ready")
        out_stored = sem("out_stored")

        QUADS = [(f, h) for h in range(2) for f in range(KF)]
        AGG = [(f, h) for f in range(KF) for h in range(2)]
        COUNT_COLS = ((0, BLK * (NB - 1)), (BLK * (NB - 1), NODES_E))
        TURNS = [[(r, s) for s in range(4)] for r in range(NB)] + [[(r, 4) for r in range(4)], [(4, 4)]]
        WT_TURNS = (range(0, 1), range(1, 4), range(4, len(TURNS)))
        LN_PARTS = ((0, 1), (2, 3), (4,))
        Y_GROUPS = [[(0, b) for b in range(4)], [(0, 4)], [(1, 0), (1, 1)], [(1, 2), (1, 3), (1, 4)]]

        groups = Groups(filled, bank)
        groups.spare = (5, 6, 7)
        groups.plan(["edges"], edge_cols_ready, 1)
        groups.plan(["vecs"], vecs_ready, 1)
        groups.plan(["dev"], flag_ready, 1)
        groups.plan([("h0", b) for b in range(NB)], h0_lo_ready, 1)
        groups.plan([("u", 0, b) for b in range(NB)], u_lo_ready, 1)
        groups.plan([("own", 0, q) for q in range(4)], own_ready, 1)
        groups.plan([("head", 0, b) for b in range(NB)], x1_added, 1)
        groups.plan([("cnt", 0)], count_rows_ready, 1)
        groups.spare, groups.turn = (4, 5, 6, 7), 0
        groups.plan([("z", 0, 0), ("z", 0, 1)], z_read, 1, banks=(0, 1))
        groups.plan([("cnt", 1)], count_rows_ready, 2)
        groups.plan([("wt", 0)], weights_t_lo, 1)
        groups.plan([("z", 0, 2), ("z", 0, 3)], z_read, 3, banks=(2, 3))
        for l in range(1, LAYERS):
            groups.plan([("u", l, b) for b in range(2)], u_lo_ready, NB * l + 1)
            groups.plan([("wt", i) for i in WT_TURNS[l]], weights_t_lo, WT_TURNS[l][0] + 1, banks=(0, 1, 2))
            groups.plan([("u", l, b) for b in range(2, NB)], u_lo_ready, NB * l + 3)
            groups.plan([("own", l, q) for q in range(4)], own_ready, 4 * l + 1, banks=(3, None, None, None))
            groups.plan([("z", l, q) for q in range(4)], z_read, 4 * l + 1, banks=range(4))
            groups.plan([("head", l, b) for b in range(NB)], x1_added, NB * l + 1, banks=(0, 1, None, 2, 3))
        groups.plan([("h4", b) for b in range(3)], h4_lo_ready, 1, banks=range(3))
        for b in range(NB):
            groups.plan([("g", b)], u_lo_ready, NB * LAYERS + b + 1)
            if b + 3 < NB:
                groups.plan([("h4", b + 3)], h4_lo_ready, b + 4, banks=((b + 3) % 4,))
        groups.plan([("agg", q) for q in range(4)], y_ready, 1, banks=range(4))
        groups.plan([("y", i) for i in range(len(Y_GROUPS))], out_ready, 1)

        rows = lambda w: w.rearrange("(c p) n -> p c n", p=P)
        raw_plan = [(0, rows(W0), None), (1, rows(W1), None), (2, rows(W2), None),
                    (0, rows(Wf)[:, 0:4, :], (w_lo_pool, 2)), (1, rows(Wf)[:, 4:8, :], (w_lo_vector, 3)),
                    (2, rows(W4), (w_lo_vector, 5))]
        LO_WB0, LO_WD0, LO_WF23, LO_W4 = [(w_lo_pool, n) for n in (1, 2, 3, 4)]
        LO_WF0, LO_W1, LO_W2, LO_WF1 = [(w_lo_vector, n) for n in (1, 3, 5, 6)]

        block = ctx.enter_context(nc.Block())

        @block.sync
        def _(sp):
            sp.dma_start(edge_rows_i[:, 0, :], src.rearrange("(t p) -> t p", p=EP)).then_inc(edges_loaded, 16)
            sp.dma_start(edge_rows_i[:, 1, :], dst.rearrange("(t p) -> t p", p=EP)).then_inc(edges_loaded, 16)
            for i, (slot, source, freed) in enumerate(raw_plan):
                if freed:
                    sp.wait_ge(*freed)
                sp.dma_start(raw[slot][:, 0:source.shape[1], :], source).then_inc(raw_loaded[slot], 16)
                if i == 0:
                    for k, v in enumerate((b0, b1, b2, b4, gamma, beta)):
                        sp.dma_start(vec_rows[KF * k:KF * k + KF, :],
                                     v.rearrange("(f p) -> f p", p=P)).then_inc(vecs_loaded, 16)
                    sp.dma_start(bf_all[:, :],
                                 bf.rearrange("(a d) -> a d", a=1).broadcast_to([BLK, D])).then_inc(bias_loaded, 16)
            for i, pairs in enumerate(Y_GROUPS):
                f, b = pairs[0]
                n = len(pairs)
                sp.wait_ge(out_ready, i + 1)
                sp.dma_start(out[BLK * b:BLK * (b + n), P * f:P * (f + 1)].rearrange("(b p) d -> p b d", p=BLK),
                             x_in[:, b:b + n, P * f:P * (f + 1)]).then_inc(out_stored, 16)
            sp.wait_ge(out_stored, 16 * len(Y_GROUPS))

        @block.gpsimd
        def _(pool):
            step = Steps(pool, pool_steps)
            step.add(pool.memset(ident[:, :], 0.0))
            step.wait()
            pool.affine_select(out=ident[:, :], in_=ident[:, :], compare_op=ALU.not_equal, fill=1.0,
                               base=0, pattern=[[-1, P]], channel_multiplier=1).then_inc(ident_ready, 1)
            pool.iota(base_id[:, :, :].rearrange("p c (a b) -> p c a b", b=3),
                      [[BLK, NB], [22, 6], [7, 3]], base=-MARGIN, channel_multiplier=0,
                      allow_small_or_imprecise_dtypes=True).then_inc(constants_ready, 1)
            pool.iota(node_id[:, :], [[1, OH]], base=0, channel_multiplier=0,
                      allow_small_or_imprecise_dtypes=True).then_inc(constants_ready, 1)
            pool.memset(eps[:, :], EPS)
            pool.memset(ones_f[:, :], 1.0)
            pool.memset(zeros_bf[:, :], 0.0)
            pool.memset(counts[:, :, NODES:NODES_E].bitcast(F32), 0.0)
            pool.memset(h0_hi[:, :, NODES:NODES_E].bitcast(F32), 0.0)
            pool.memset(h0_lo[:, :, NODES:NODES_E].bitcast(F32), 0.0).then_inc(constants_ready, 1)

            pool.wait_ge(edge_cols_ready, 1)
            w = edge_cols[:, 2, :]
            for k in range(3):
                pool.tensor_copy(weight_parts[:, k, :], w).then_inc(weight_part_ready, 1)
                pool.wait_ge(weight_part_ready, k + 1)
                if k < 2:
                    step.add(pool.tensor_tensor(weight_rest[:, k, :], w, weight_parts[:, k, :], ALU.subtract))
                    step.wait()
                    w = weight_rest[:, k, :]

            def weighted_windows(c, first=1):
                pool.wait_ge(window_ready, c + 1)
                hot = dst_hot[:, PER * c:PER * (c + 1), :, :]
                for k in range(first, KINDS):
                    part = weight_parts[:, k - 1, PER * c:PER * (c + 1)].unsqueeze(2).to_broadcast([EP, PER, WINDOW])
                    ins = pool.tensor_tensor(hot[:, :, k, :], hot[:, :, 0, :], part, ALU.mult)
                ins.then_inc(weighted_windows_ready, 1)

            def difference(l):
                r = raw[l]
                pool.wait_ge(raw_loaded[l], 16)
                pool.tensor_tensor(r[:, 0:KF, :], r[:, 0:KF, :], r[:, KF:2 * KF, :], ALU.subtract).then_inc(w_diff, 1)

            def low_part(n_hi, lo, source, hi):
                pool.wait_ge(w_hi, n_hi)
                pool.tensor_tensor(lo, source, hi.bitcast(F32), ALU.subtract).then_inc(w_lo_pool, 1)

            def sum_weights(g):
                r, s = divmod(g, NB)
                pool.wait_ge(block_copied, g + 1)
                part = stage[:, g % STAGES, :, :]
                step.add(pool.tensor_tensor(part[:, 1, :], part[:, 1, :], part[:, 2, :], ALU.add))
                step.wait()
                pool.tensor_tensor(weights[:, s, BLK * r:BLK * (r + 1)], part[:, 0, :], part[:, 1, :],
                                   ALU.add).then_inc(weights_summed, 1)

            def mask_own(l, h):
                a, e = HALVES[h]
                if l == 0:
                    pool.wait_ge(has_edge_ready, h + 1)
                for f in range(KF):
                    pool.wait_ge(own_ready, 4 * l + KF * h + f + 1)
                    pool.tensor_tensor(own[:, f, a:e], own[:, f, a:e], has_edge[:, a:e],
                                       ALU.mult).then_inc(own_masked, 1)

            difference(0)
            weighted_windows(0, first=2)
            low_part(1, wb[0][1][:, :, :], raw[0][:, KF:2 * KF, :], wb[0][0][:, :, :])
            weighted_windows(1)
            pool.wait_ge(bias_loaded, 16)
            pool.wait_ge(h0_ready, NB)
            pool.wait_ge(norm_ready, 1)
            pool.tensor_tensor(x_in[:, :, :], x_in[:, :, :],
                               bf_all[:, :].unsqueeze(1).to_broadcast([BLK, NB, D]), ALU.add).then_inc(xb_ready, 1)
            low_part(2, wd[0][1][:, :, :], raw[0][:, 0:KF, :], wd[0][0][:, :, :])
            weighted_windows(2)
            difference(1)
            difference(2)
            for g in range(NB * NB):
                sum_weights(g)
                if g == 4:
                    weighted_windows(3)
                if g == 9:
                    weighted_windows(4)
                if g == 19:
                    mask_own(0, 0)
            pool.wait_ge(block_built, NB * NB)
            pool.memset(weights_hi[:, :, NODES:NODES_E].bitcast(F32), 0.0)
            pool.memset(weights_lo[:, :, NODES:NODES_E].bitcast(F32), 0.0).then_inc(constants_ready, 1)
            mask_own(0, 1)
            low_part(9, wf23_lo[:, :, :], raw[1][:, :, :], wf23_hi[:, :, :])
            low_part(10, w4[1][:, :, :], raw[2][:, 0:KF, :], w4[0][:, :, :])
            for l in range(1, LAYERS):
                mask_own(l, 0)
                mask_own(l, 1)

        @block.vector
        def _(dve):
            step = Steps(dve, vector_steps)
            dve.wait_ge(edges_loaded, 32)
            dve.tensor_copy(edge_rows[:, 0:2, :], edge_rows_i[:, :, :]).then_inc(edge_rows_ready, 1)
            stds = [0]

            summed = {}

            def moments_of(b):
                summed[b] = step.add(dve.bn_stats(stats[0:BLK, b, :], x_in[:, b, :]))

            def variances(blocks):
                for b in blocks:
                    step.wait(summed[b])
                    last = dve.bn_aggr(moments[0:BLK, b, :], stats[0:BLK, b, :])
                last.then_inc(variance_ready, 1)

            def scale_shift(blocks, ready):
                stds[0] += 1
                dve.wait_ge(std_ready, stds[0])
                lo, hi = blocks[0], blocks[-1] + 1
                step.add(dve.reciprocal(rstd[0:BLK, lo:hi], rstd[0:BLK, lo:hi]))
                step.wait()
                dve.scalar_tensor_tensor(out=shift[0:BLK, lo:hi], in0=moments[0:BLK, lo:hi, 0], scalar=-1.0,
                                         in1=rstd[0:BLK, lo:hi], op0=ALU.mult, op1=ALU.mult).then_inc(ready, 1)

            groups.wait_filled(dve, "edges")
            e3 = groups.bank["edges"][0:EP, 0:3 * TILES].rearrange("p (v t) -> p v t", v=3)
            dve.tensor_copy(edge_cols[:, :, :], e3).then_inc(edge_cols_ready, 1)
            dve.wait_ge(edge_cols_ready, 1)
            dve.wait_ge(constants_ready, 1)
            step.add(dve.tensor_tensor(rel[:, :, :], edge_cols[:, 1, :].rearrange("p (c j) -> p c j", c=NB),
                                       base_id[:, :, 0:PER], ALU.subtract))
            step.wait()
            dve.wait_ge(constants_ready, 3)

            def plain_window(c):
                hot = dst_hot[:, PER * c:PER * (c + 1), :, :]
                ids = node_id[:, 0:WINDOW].unsqueeze(1).to_broadcast([EP, PER, WINDOW])
                at = rel[:, c, :].unsqueeze(2).to_broadcast([EP, PER, WINDOW])
                dve.tensor_tensor(hot[:, :, 0, :], ids, at, ALU.is_equal).then_inc(window_ready, 1)

            def high_window(c):
                hot = dst_hot[:, PER * c:PER * (c + 1), :, :]
                dve.wait_ge(weight_part_ready, 1)
                dve.wait_ge(window_ready, c + 1)
                part = weight_parts[:, 0, PER * c:PER * (c + 1)].unsqueeze(2).to_broadcast([EP, PER, WINDOW])
                dve.tensor_tensor(hot[:, :, 1, :], hot[:, :, 0, :], part, ALU.mult).then_inc(high_window_ready, 1)

            def source_tile(t):
                if t not in SCALAR_TILES:
                    dve.tensor_scalar(src_hot[:, t % RING, :], node_id[:, :], edge_cols[:, 0, t:t + 1], None,
                                      ALU.is_equal).then_inc(src_hot_vector, 1)

            dve.wait_ge(x_loaded, 16)
            for b in range(NB):
                moments_of(b)
            variances(range(NB))
            plain_window(0)
            scale_shift(range(NB), norm_ready)
            groups.wait_filled(dve, "vecs")
            dve.tensor_copy(vecs[:, :], groups.bank["vecs"][:, 0:6 * KF]).then_inc(vecs_ready, 1)
            step.add(dve.tensor_scalar(dev[:, :], rel[:, :, :].rearrange("p c j -> p (c j)"),
                                       (WINDOW - 1) / 2, None, ALU.subtract))
            step.wait()
            dve.tensor_reduce(dev_max[:, :], dev[:, :], AX.X, ALU.max, apply_absolute_value=True).then_inc(dev_ready, 1)
            source_tile(1)
            groups.wait_filled(dve, "dev")
            step.add(dve.tensor_reduce(worst[:, :], groups.bank["dev"][0:1, 0:EP], AX.X, ALU.max))
            step.wait()
            dve.tensor_scalar(flag[:, :], worst[:, :], WINDOW / 2, None, ALU.is_gt).then_inc(flag_ready, 1)
            high_window(0)
            plain_window(1)

            def low_rows(name, b, n):
                dve.wait_ge(u_hi_ready, n)
                dve.tensor_tensor(u_lo[:, b, :], groups.bank[name][0:BLK, 0:D], u_hi[:, b, :].bitcast(F32),
                                  ALU.subtract).then_inc(u_lo_ready, 1)

            made = 2
            for b in range(NB):
                dve.wait_ge(h_hi_ready, b + 1)
                t2 = groups.bank[("h0", b)][:, 0:KF * BLK].rearrange("p (f n) -> p f n", f=KF)
                cols = slice(BLK * b, BLK * (b + 1))
                dve.tensor_tensor(h0_lo[:, :, cols], t2, h0_hi[:, :, cols].bitcast(F32),
                                  ALU.subtract).then_inc(h0_lo_ready, 1)
                for t in range(made, made + 1 + (b in (2, 3))):
                    source_tile(t)
                    made += 1
            plain_window(2)
            for b in range(NB):
                for t in range(made, made + 2):
                    source_tile(t)
                made += 2
                low_rows(("u", 0, b), b, b + 1)
            assert made == PRE
            plain_window(3)
            plain_window(4)
            dve.tensor_copy(ones_r[:, :], ones_f[:, :]).then_inc(ones_ready, 1)

            def low_part(n_hi, lo, source, hi):
                dve.wait_ge(w_hi, n_hi)
                dve.tensor_tensor(lo, source, hi.bitcast(F32), ALU.subtract).then_inc(w_lo_vector, 1)

            def low_parts(i):
                if i == 0:
                    low_part(3, wf01[1][:, 0:KF, :], raw[0][:, 0:KF, :], wf01[0][:, 0:KF, :])
                if i in (1, 2):
                    low_part(2 * i + 2, wb[i][1][:, :, :], raw[i][:, KF:2 * KF, :], wb[i][0][:, :, :])
                    low_part(2 * i + 3, wd[i][1][:, :, :], raw[i][:, 0:KF, :], wd[i][0][:, :, :])
                if i == 2:
                    low_part(8, wf01[1][:, KF:2 * KF, :], raw[0][:, KF:2 * KF, :], wf01[0][:, KF:2 * KF, :])

            def count_rows(i):
                a, e = COUNT_COLS[i]
                c = groups.bank[("cnt", i)][:, 0:e - a]
                if i == 0:
                    dve.wait_ge(block_built, NB * 3)
                    dve.wait_ge(weighted_windows_ready, 2)
                groups.wait_filled(dve, ("cnt", i))
                dve.tensor_scalar(has_edge[:, a:e], c, 1.0, None, ALU.min).then_inc(has_edge_ready, 1)
                dve.tensor_scalar(inv_count[:, a:e], c, 1.0, None, ALU.max).then_inc(counts_bounded, 1)
                dve.wait_ge(counts_bounded, i + 1)
                dve.reciprocal(inv_count[:, a:e], inv_count[:, a:e]).then_inc(count_rows_ready, 1)

            def add_head(l, b):
                if l == 0 and b == 0:
                    dve.wait_ge(xb_ready, 1)
                groups.wait_filled(dve, ("head", l, b))
                dve.wait_ge(x1_added, NB * (l - 1) + b + 1) if l else None
                dve.tensor_tensor(x_in[:, b, :], x_in[:, b, :], groups.bank[("head", l, b)][0:BLK, 0:D],
                                  ALU.add).then_inc(x1_added, 1)

            dve.wait_ge(flag_ready, 1)
            general = dve.value_load(flag[0:1, 0:1], min_val=0, max_val=1)
            with dve.If(general > 0):
                dve.wait_ge(weight_part_ready, 3)
                dve.tensor_copy(parts_f[:, :, :], weight_parts[:, :, :]).then_inc(parts_ready, 1)
                dve.wait_ge(parts_ready, 1)
                for r in range(NB):
                    with dve.Fori(0, PER) as j:
                        for i in range(SLOW):
                            t = j * SLOW + i
                            dve.wait_ge(slow_slot_free, t + (TILES * r + 1))
                            dve.tensor_scalar(src_hot[:, i, :], node_id[:, :], edge_cols[:, 0, bass.ds(t, 1)], None,
                                              ALU.is_equal)
                            hot = src_hot[:, 2 * PER + i, 0:KINDS * BLK].rearrange("p (k n) -> p k n", k=KINDS)
                            ids = node_id[:, BLK * r:BLK * (r + 1)]
                            at = edge_cols[:, 1, bass.ds(t, 1)]
                            dve.tensor_scalar(hot[:, 0, :], ids, at, None, ALU.is_equal)
                            for k in range(3):
                                ins = dve.tensor_scalar(hot[:, k + 1, :], ids, at, parts_f[:, k, bass.ds(t, 1)],
                                                        ALU.is_equal, ALU.mult)
                            ins.then_inc(slow_slot_ready, 1)
                    for s in range(NB):
                        g = NB * r + s
                        dve.wait_ge(block_copied, g + 1)
                        at = slice(BLK * r, BLK * (r + 1))
                        dve.tensor_tensor(counts_lo[:, s, at], built[s][0:BLK, 0, 0:BLK],
                                          counts[:, s, at].bitcast(F32), ALU.subtract).then_inc(block_rest, 1)
                    if r == 0:
                        low_parts(0)
                    if r == 1:
                        for b in range(NB):
                            add_head(0, b)
                dve.memset(counts_lo[:, :, NODES:NODES_E].bitcast(F32), 0.0).then_inc(block_rest, 1)
            with dve.Else():
                for t in range(PRE, TILES):
                    if t >= RING:
                        dve.wait_ge(block_built, NB * (last_block(t - RING) + 1))
                    source_tile(t)
                    if t == LOW_AFTER:
                        low_parts(0)
                    if HEAD_AFTER <= t < HEAD_AFTER + NB:
                        add_head(0, t - HEAD_AFTER)
            low_parts(1)
            low_parts(2)
            count_rows(0)

            def turned(i, t):
                b, pairs = groups.bank[("wt", i)], TURNS[i]
                r, s = pairs[0]
                if len(pairs) == 1:
                    return b[0:BLK, 0:BLK], t[:, r, BLK * s:BLK * (s + 1)]
                if pairs[1][0] == r:
                    return b[0:BLK, 0:4 * BLK], t[:, r, BLK * s:BLK * (s + 4)]
                return b[0:BLK, 0:4 * BLK].rearrange("p (r n) -> p r n", r=4), t[:, r:r + 4, BLK * s:BLK * (s + 1)]

            def z_step(l, q):
                f, h = QUADS[q]
                a, e = HALVES[h]
                n = 4 * l + q + 1
                groups.wait_filled(dve, ("z", l, q))
                if l == 0 and f == 0:
                    dve.wait_ge(count_rows_ready, h + 1)
                dve.tensor_tensor(pre_t[:, f, a:e], groups.bank[("z", l, q)][:, 0:e - a], inv_count[:, a:e],
                                  ALU.mult).then_inc(z_read, 1)
                dve.wait_ge(z_read, n)
                dve.wait_ge(own_masked, n)
                dve.tensor_tensor(pre_t[:, f, a:e], pre_t[:, f, a:e], own[:, f, a:e], ALU.add).then_inc(z_ready, 1)

            def h_low(l, q):
                f, h = QUADS[q]
                a, e = HALVES[h]
                dve.wait_ge(h_hi_ready, NB + 4 * l + q + 1)
                dve.scalar_tensor_tensor(out=h_lo[l + 1][:, f, a:e], in0=pre_t[:, f, a:e], scalar=0.0,
                                         in1=h_hi[l + 1][:, f, a:e].bitcast(F32), op0=ALU.max,
                                         op1=ALU.subtract).then_inc(h_lo_ready, 1)

            def turned_low(i):
                dve.wait_ge(weights_t_hi, i + 1)
                p, lo = turned(i, weights_lo)
                dve.tensor_tensor(lo, p, turned(i, weights_hi)[1].bitcast(F32), ALU.subtract).then_inc(weights_t_lo, 1)

            for l in range(LAYERS):
                if l >= 1:
                    for b in range(NB):
                        if b == 3:
                            for i in WT_TURNS[l]:
                                turned_low(i)
                        low_rows(("u", l, b), b, NB * l + b + 1)
                z_step(l, 0)
                z_step(l, 1)
                if l == 0:
                    count_rows(1)
                h_low(l, 0)
                h_low(l, 1)
                z_step(l, 2)
                z_step(l, 3)
                h_low(l, 2)
                h_low(l, 3)
                if l == 0:
                    turned_low(0)
                if l == 1:
                    for b in range(NB):
                        add_head(l, b)

            def h4_low(b):
                dve.wait_ge(h4_hi_ready, b + 1)
                t2 = groups.bank[("h4", b)][:, 0:KF * BLK].rearrange("p (f n) -> p f n", f=KF)
                cols = slice(BLK * b, BLK * (b + 1))
                dve.tensor_tensor(h4_lo[:, :, cols], t2, h4_hi[:, :, cols].bitcast(F32),
                                  ALU.subtract).then_inc(h4_lo_ready, 1)

            def moments_of_sum(b):
                dve.wait_ge(x1_added, NB * (LAYERS - 1) + b + 1)
                moments_of(b)

            first, second, third = LN_PARTS
            for b in first:
                add_head(LAYERS - 1, b)
            for b in first:
                moments_of_sum(b)
            variances(first)
            add_head(LAYERS - 1, 2)
            scale_shift(first, norm4_ready)
            add_head(LAYERS - 1, 3)
            for b in second:
                moments_of_sum(b)
            variances(second)
            add_head(LAYERS - 1, 4)
            scale_shift(second, norm4_ready)
            moments_of_sum(4)
            variances(third)
            h4_low(0)
            h4_low(1)
            scale_shift(third, norm4_ready)
            g_low = lambda b: low_rows(("g", b), b, NB * LAYERS + b + 1)
            h4_low(2)
            for b in range(NB):
                if b + 3 < NB:
                    h4_low(b + 3)
                g_low(b)
            vec = lambda k, f: vecs[:, KF * k + f:KF * k + f + 1]
            for f in range(KF):
                for h, (a, e) in enumerate(HALVES):
                    q = AGG.index((f, h))
                    groups.wait_filled(dve, ("agg", q))
                    step.add(dve.bn_stats(stats[:, 2 * f + h, :], groups.bank[("agg", q)][:, 0:min(e, NODES) - a]))
                step.wait()
                stds[0] += 1
                dve.bn_aggr(moments[:, f, :],
                            stats[:, 2 * f:2 * f + 2, :].rearrange("p a b -> p (a b)")).then_inc(variance_ready, 1)
                dve.wait_ge(variance_ready, stds[0])
                step.add(dve.tensor_tensor(shift[:, f:f + 1], moments[:, f, 0:1], vec(3, f), ALU.add))
                step.wait()
                step.add(dve.tensor_tensor(shift[:, f:f + 1], vec(3, f), shift[:, f:f + 1], ALU.subtract))
                step.wait()
                step.add(dve.tensor_tensor(shift[:, f:f + 1], shift[:, f:f + 1], vec(4, f), ALU.mult))
                dve.wait_ge(std_ready, stds[0])
                step.add(dve.reciprocal(rstd[:, f:f + 1], rstd[:, f:f + 1]))
                step.wait()
                dve.scalar_tensor_tensor(out=shift[:, f:f + 1], in0=shift[:, f:f + 1], scalar=rstd[:, f:f + 1],
                                         in1=vec(5, f), op0=ALU.mult, op1=ALU.add)
                dve.tensor_tensor(scale[:, f:f + 1], rstd[:, f:f + 1], vec(4, f), ALU.mult).then_inc(bn_ready, 1)
            for i, pairs in enumerate(Y_GROUPS):
                f, b = pairs[0]
                n = len(pairs)
                groups.wait_filled(dve, ("y", i))
                o = x_in[:, b:b + n, P * f:P * (f + 1)]
                dve.tensor_tensor(o, o, groups.bank[("y", i)][0:BLK, 0:P * n].rearrange("p (b d) -> p b d", b=n),
                                  ALU.add).then_inc(out_ready, 1)

        @block.scalar
        def _(act):
            act.dma_start(edge_rows[:, 2, :],
                          edge_weight.rearrange("(t p) -> t p", p=EP)).then_inc(edge_weights_loaded, 16)
            act.dma_start(x_in[:, :, :], x.rearrange("(b p) d -> p b d", p=BLK)).then_inc(x_loaded, 16)
            copy = lambda o, i: nc.scalar.activation(o, i, ACT.Copy)
            stds = [0]
            act.wait_ge(ident_ready, 1)
            nc.scalar.activation(root_table[:, :], ident[0:1, 0:1], ACT.Sqrt)

            def root(o, variance):
                stds[0] += 1
                act.wait_ge(variance_ready, stds[0])
                nc.scalar.activation(o, variance, ACT.Sqrt, bias=eps[0:o.shape[0], :]).then_inc(std_ready, 1)

            def high_part(o, i):
                copy(o, i).then_inc(w_hi, 1)

            tiles_made = [0]

            def source_tile(t):
                if tiles_made[0]:
                    act.wait_ge(src_hot_scalar, tiles_made[0])
                tiles_made[0] += 1
                nc.scalar.activation(distance[:, :], node_id[:, :], ACT.Abs, bias=edge_cols[:, 0, t:t + 1],
                                     scale=-1.0).then_inc(distance_ready, 1)
                act.wait_ge(distance_ready, tiles_made[0])
                nc.scalar.activation(src_hot[:, t % RING, :], distance[:, :], ACT.Relu, bias=1.0,
                                     scale=-1.0).then_inc(src_hot_scalar, 1)

            def high_rows(name, b):
                groups.wait_filled(act, name)
                copy(u_hi[:, b, :], groups.bank[name][0:BLK, 0:D]).then_inc(u_hi_ready, 1)

            def own_terms(l, quads=range(4)):
                for q in quads:
                    f, h = QUADS[q]
                    a, e = HALVES[h]
                    groups.wait_filled(act, ("own", l, q))
                    if l >= 1:
                        act.wait_ge(z_ready, 4 * (l - 1) + q + 1)
                    nc.scalar.activation(own[:, f, a:e], groups.bank[("own", l, q)][:, 0:e - a], ACT.Identity,
                                         bias=vecs[:, KF * l + f:KF * l + f + 1]).then_inc(own_ready, 1)

            act.wait_ge(edge_cols_ready, 1)
            act.wait_ge(constants_ready, 3)
            source_tile(0)
            act.wait_ge(raw_loaded[0], 16)
            high_part(wb[0][0][:, :, :], raw[0][:, KF:2 * KF, :])

            def h0_high(b):
                groups.wait_filled(act, ("h0", b))
                t2 = groups.bank[("h0", b)][:, 0:KF * BLK].rearrange("p (f n) -> p f n", f=KF)
                copy(h0_hi[:, :, BLK * b:BLK * (b + 1)], t2).then_inc(h_hi_ready, 1)

            root(rstd[0:BLK, 0:NB], moments[0:BLK, 0:NB, 1])
            act.wait_ge(norm_ready, 1)
            for b in range(NB):
                nc.scalar.activation(h0[:, b, :], x_in[:, b, :], ACT.Relu, bias=shift[0:BLK, b:b + 1],
                                     scale=rstd[0:BLK, b:b + 1]).then_inc(h0_ready, 1)
                if b >= 2:
                    h0_high(b - 2)
            source_tile(6)
            h0_high(3)
            h0_high(4)
            source_tile(10)
            high_rows(("u", 0, 0), 0)
            act.wait_ge(w_diff, 1)
            high_part(wd[0][0][:, :, :], raw[0][:, 0:KF, :])
            for b in range(1, NB):
                high_rows(("u", 0, b), b)
            act.wait_ge(vecs_ready, 1)

            def copy_block(g):
                r, s = divmod(g, NB)
                act.wait_ge(block_built, g + 1)
                if g >= STAGES:
                    act.wait_ge(weights_summed, g - STAGES + 1)
                copy(counts[:, s, BLK * r:BLK * (r + 1)], built[g % NB][0:BLK, 0, 0:BLK])
                copy(stage[:, g % STAGES, :, :], built[g % NB][0:BLK, 1:KINDS, 0:BLK]).then_inc(block_copied, 1)

            for r in range(NB):
                for s in range(NB):
                    copy_block(NB * r + s)
                    if r == 0 and s:
                        own_terms(0, (s - 1,))
                if r == 0:
                    act.wait_ge(raw_loaded[0], 32)
                    high_part(wf01[0][:, 0:KF, :], raw[0][:, 0:KF, :])
                    act.wait_ge(w_diff, 3)
                for t in SCALAR_LATER.get(r, ()):
                    if t >= RING:
                        act.wait_ge(block_built, NB * (last_block(t - RING) + 1))
                    source_tile(t)
                if r in (1, 2):
                    high_part(wb[r][0][:, :, :], raw[r][:, KF:2 * KF, :])
                    high_part(wd[r][0][:, :, :], raw[r][:, 0:KF, :])
                if r == 2:
                    high_part(wf01[0][:, KF:2 * KF, :], raw[0][:, KF:2 * KF, :])

            act.wait_ge(raw_loaded[1], 32)
            high_part(wf23_hi[:, :, :], raw[1][:, :, :])

            def turned(i):
                b, pairs = groups.bank[("wt", i)], TURNS[i]
                r, s = pairs[0]
                if len(pairs) == 1:
                    return b[0:BLK, 0:BLK], weights_hi[:, r, BLK * s:BLK * (s + 1)]
                if pairs[1][0] == r:
                    return b[0:BLK, 0:4 * BLK], weights_hi[:, r, BLK * s:BLK * (s + 4)]
                return (b[0:BLK, 0:4 * BLK].rearrange("p (r n) -> p r n", r=4),
                        weights_hi[:, r:r + 4, BLK * s:BLK * (s + 1)])

            def turned_high(i):
                groups.wait_filled(act, ("wt", i))
                p, hi = turned(i)
                copy(hi, p).then_inc(weights_t_hi, 1)

            for l in range(LAYERS):
                if l >= 1:
                    for b in range(NB):
                        if b == 3:
                            for i in WT_TURNS[l]:
                                turned_high(i)
                        high_rows(("u", l, b), b)
                    own_terms(l)
                for q, (f, h) in enumerate(QUADS):
                    a, e = HALVES[h]
                    if l == 0 and q == 2:
                        turned_high(0)
                    act.wait_ge(z_ready, 4 * l + q + 1)
                    nc.scalar.activation(h_hi[l + 1][:, f, a:e], pre_t[:, f, a:e], ACT.Relu).then_inc(h_hi_ready, 1)
                if l == 0:
                    act.wait_ge(raw_loaded[2], 32)
                    high_part(w4[0][:, :, :], raw[2][:, 0:KF, :])
            act.wait_ge(h_lo_ready, 4 * LAYERS)
            def h4_high(b):
                groups.wait_filled(act, ("h4", b))
                t2 = groups.bank[("h4", b)][:, 0:KF * BLK].rearrange("p (f n) -> p f n", f=KF)
                copy(h4_hi[:, :, BLK * b:BLK * (b + 1)], t2).then_inc(h4_hi_ready, 1)

            def h4_row(b):
                nc.scalar.activation(h4_rows[:, b, :], x_in[:, b, :], ACT.Relu, bias=shift[0:BLK, b:b + 1],
                                     scale=rstd[0:BLK, b:b + 1]).then_inc(h4_rows_ready, 1)

            def root4(n):
                part = LN_PARTS[n]
                root(rstd[0:BLK, part[0]:part[-1] + 1], moments[0:BLK, part[0]:part[-1] + 1, 1])

            root4(0)
            act.wait_ge(norm4_ready, 1)
            h4_row(0)
            h4_row(1)
            root4(1)
            h4_high(0)
            h4_high(1)
            act.wait_ge(norm4_ready, 2)
            h4_row(2)
            root4(2)
            h4_row(3)
            h4_high(2)
            act.wait_ge(norm4_ready, 3)
            h4_row(4)
            for b in range(NB):
                if b + 3 < NB:
                    h4_high(b + 3)
                high_rows(("g", b), b)
            for f in range(KF):
                root(rstd[:, f:f + 1], moments[:, f, 1:2])
                act.wait_ge(bn_ready, f + 1)
                for h, (a, e) in enumerate(HALVES):
                    e = min(e, NODES)
                    q = AGG.index((f, h))
                    nc.scalar.activation(pre_t[:, f, a:e], groups.bank[("agg", q)][:, 0:e - a], ACT.Relu,
                                         bias=shift[:, f:f + 1], scale=scale[:, f:f + 1]).then_inc(y_ready, 1)

        @block.tensor
        def _(pe):
            def three(o, lhs, rhs, start, stop):
                (lh, ll), (rh, rl) = lhs, rhs
                pe.matmul(o, lh, rh, start=start, stop=False)
                pe.matmul(o, ll, rh, start=False, stop=False)
                return pe.matmul(o, lh, rl, start=False, stop=stop)

            def fill(name):
                groups.wait_free(pe, name)
                return groups.bank[name]

            def keep_warm(n):
                for _ in range(n):
                    pe.matmul(bank[4][:, :], zeros_bf[:, :], node_id[:, 0:512], start=True, stop=True)

            pe.wait_ge(ident_ready, 1)
            pe.wait_ge(edge_rows_ready, 1)
            pe.wait_ge(edge_weights_loaded, 16)
            e3 = fill("edges")
            for v in range(3):
                ins = pe.transpose(e3[0:EP, TILES * v:TILES * (v + 1)], edge_rows[:, v, :], ident[0:TILES, 0:TILES])
            ins.then_inc(filled, 1)
            pe.wait_ge(constants_ready, 3)
            keep_warm(4)
            pe.wait_ge(vecs_loaded, 16 * 6)
            pe.transpose(fill("vecs")[:, 0:6 * KF], vec_rows[:, :], ident[0:6 * KF, 0:6 * KF]).then_inc(filled, 1)
            keep_warm(4)
            pe.wait_ge(dev_ready, 1)
            pe.transpose(fill("dev")[0:1, 0:EP], dev_max[:, :], ident[0:EP, 0:EP]).then_inc(filled, 1)

            def turn_h0(b):
                pe.wait_ge(h0_ready, b + 1)
                o = fill(("h0", b))
                for f in range(KF):
                    ins = pe.transpose(o[:, BLK * f:BLK * (f + 1)], h0[:, b, P * f:P * (f + 1)], ident[0:BLK, 0:BLK])
                ins.then_inc(filled, 1)

            def project(name, lhs, rhs, opens=True, closes=True):
                o = fill(name) if opens else groups.bank[name]
                for k in range(len(lhs)):
                    ins = three(o[0:BLK, 0:D], lhs[k], rhs[k], opens and k == 0, closes and k == len(lhs) - 1)
                if closes:
                    ins.then_inc(filled, 1)

            def feature_rows(hi, lo, b):
                return [(hi[:, k, BLK * b:BLK * (b + 1)], lo[:, k, BLK * b:BLK * (b + 1)]) for k in range(KF)]

            def neighbour_terms(l, blocks=range(NB)):
                for b in blocks:
                    if l == 0:
                        pe.wait_ge(h0_lo_ready, b + 1)
                        pe.wait_ge(*LO_WB0)
                    elif b in (0, 2):
                        pe.wait_ge(h_lo_ready, 4 * (l - 1) + (2 if b == 0 else 4))
                    project(("u", l, b), feature_rows(h_hi[l], h_lo[l], b),
                            [(wb[l][0][:, k, :], wb[l][1][:, k, :]) for k in range(KF)])

            def own_terms(l):
                for q, (f, h) in enumerate(QUADS):
                    a, e = HALVES[h]
                    o = fill(("own", l, q))
                    fc = slice(P * f, P * (f + 1))
                    for k in range(KF):
                        ins = three(o[:, 0:e - a], (wd[l][0][:, k, fc], wd[l][1][:, k, fc]),
                                    (h_hi[l][:, k, a:e], h_lo[l][:, k, a:e]), k == 0, k == KF - 1)
                    ins.then_inc(filled, 1)

            def head(l, blocks=range(NB)):
                (wh, c), (wl, _) = wf_of(l, 0), wf_of(l, 1)
                for b in blocks:
                    if l == LAYERS and b in (0, 2):
                        pe.wait_ge(h_lo_ready, 4 * (l - 1) + (2 if b == 0 else 4))
                    project(("head", min(l, LAYERS - 1), b), feature_rows(h_hi[l], h_lo[l], b),
                            [(wh[:, c + k, :], wl[:, c + k, :]) for k in range(KF)],
                            opens=(l < LAYERS), closes=(l != LAYERS - 1))

            def count_sums(i, a, e, low):
                pe.wait_ge(ones_ready, 1)
                o = groups.bank[("cnt", i)][:, a - COUNT_COLS[i][0]:e - COUNT_COLS[i][0]]
                parts = [counts, counts_lo] if low else [counts]
                pe.wait_ge(block_copied, NB * ((e - 1) // BLK + 1) if e < NODES else NB * NB)
                for part in parts:
                    for s in range(NB):
                        ins = pe.matmul(o, ones_r[:, :], part[:, s, a:e], start=(s == 0 and part is counts),
                                        stop=(s == NB - 1 and part is parts[-1]), skip_group_check=True)
                return ins

            turn_h0(0)
            turn_h0(1)
            turn_h0(2)
            keep_warm(2)
            jobs = {0: lambda: turn_h0(3), 1: lambda: turn_h0(4), 3: lambda: neighbour_terms(0, (0,)),
                    5: lambda: neighbour_terms(0, (1,)), 7: lambda: neighbour_terms(0, (2,)),
                    9: lambda: neighbour_terms(0, (3,)), 11: lambda: neighbour_terms(0, (4,))}

            def between(r):
                if r == 0:
                    pe.wait_ge(*LO_WD0)
                    own_terms(0)
                if r == 1:
                    pe.wait_ge(*LO_WF0)
                    head(0)

            pe.wait_ge(flag_ready, 1)
            general = pe.value_load(flag[0:1, 0:1], min_val=0, max_val=1)
            with pe.If(general > 0):
                for job in jobs.values():
                    job()
                pe.wait_ge(src_hot_vector, PRE - len(SCALAR_EARLY))
                pe.wait_ge(src_hot_scalar, len(SCALAR_EARLY))
                for i in range(SLOW):
                    pe.matmul(bank[0][:, 0:P], zeros_bf[:, :], zeros_bf[:, :],
                              start=True, stop=True).then_inc(slow_slot_free, 1)
                for r in range(NB):
                    for s in range(NB):
                        if r:
                            pe.wait_ge(block_rest, NB * (r - 1) + s + 1)
                        pe.matmul(bank[s][:, :], zeros_bf[:, :], node_id[:, 0:512], start=True, stop=False,
                                  skip_group_check=True)
                    with pe.Fori(0, PER) as j:
                        for i in range(SLOW):
                            pe.wait_ge(slow_slot_ready, j * SLOW + (TILES * r + i + 1))
                            hot = src_hot[:, 2 * PER + i, 0:KINDS * BLK].rearrange("p (k n) -> p k n", k=KINDS)
                            for s in range(NB):
                                ins = pe.matmul(built[s][:, :, 0:BLK], src_hot[:, i, BLK * s:BLK * s + P], hot,
                                                start=False, stop=False, skip_group_check=True)
                            ins.then_inc(slow_slot_free, 1)
                    for s in range(NB):
                        pe.matmul(built[s][:, :, 0:BLK], zeros_bf[:, :],
                                  node_id[:, 0:KINDS * BLK].rearrange("p (k n) -> p k n", k=KINDS),
                                  start=False, stop=True, skip_group_check=True).then_inc(block_built, 1)
                    between(r)
                pe.wait_ge(block_rest, NB * NB + 1)
                fill(("cnt", 0))
                count_sums(0, *COUNT_COLS[0], True).then_inc(filled, 1)
            with pe.Else():
                made = [0, 0]

                def wait_tile(t):
                    made[t in SCALAR_TILES] += 1
                    if t in SCALAR_TILES:
                        pe.wait_ge(src_hot_scalar, made[1])
                    else:
                        pe.wait_ge(src_hot_vector, made[0])
                    if t % PER == 0:
                        pe.wait_ge(high_window_ready, 1)
                        pe.wait_ge(weighted_windows_ready, t // PER + 1)

                seen = 0
                for r in range(NB):
                    pieces = window_pieces(r)

                    def place(s, i):
                        t, c0, n0, n = pieces[i]
                        return pe.matmul(built[s][:, :, n0:n0 + n], src_hot[:, t % RING, BLK * s:BLK * s + P],
                                         dst_hot[:, t, :, c0:c0 + n], start=(i == 0), stop=(i == len(pieces) - 1),
                                         skip_group_check=True)

                    if r <= 2:
                        for i in range(len(pieces)):
                            if r == 0 and i in jobs:
                                jobs[i]()
                            if pieces[i][0] >= seen:
                                wait_tile(seen)
                                seen += 1
                            for s in range(NB):
                                if r and i == 0:
                                    pe.wait_ge(block_copied, NB * (r - 1) + s + 1)
                                ins = place(s, i)
                                if i == len(pieces) - 1:
                                    ins.then_inc(block_built, 1)
                    else:
                        for s in range(NB):
                            pe.wait_ge(block_copied, NB * (r - 1) + s + 1)
                            for i in range(len(pieces)):
                                if pieces[i][0] >= seen:
                                    wait_tile(seen)
                                    seen += 1
                                ins = place(s, i)
                            ins.then_inc(block_built, 1)
                            if r == NB - 1 and s == 1:
                                count_sums(0, 2 * BLK, 4 * BLK, False).then_inc(filled, 1)
                    between(r)
                    if r == 2:
                        fill(("cnt", 0))
                        count_sums(0, 0, 2 * BLK, False)

            def sums(l, h):
                a, e = HALVES[h]
                quads = [(f, KF * h + f) for f in range(KF)]
                pe.wait_ge(u_lo_ready, NB * l + 1)
                for f, q in quads:
                    pe.matmul(fill(("z", l, q))[:, 0:e - a], u_hi[:, 0, P * f:P * (f + 1)], counts[:, 0, a:e],
                              start=True, stop=False, skip_group_check=True)
                with pe.If(general > 0):
                    pe.wait_ge(u_lo_ready, NB * (l + 1))
                    for f, q in quads:
                        for k in range(NB):
                            for u in (u_hi, u_lo):
                                pe.matmul(bank[q][:, 0:e - a], u[:, k, P * f:P * (f + 1)], counts_lo[:, k, a:e],
                                          start=False, stop=False, skip_group_check=True)
                for k in range(NB):
                    if h == 0:
                        pe.wait_ge(u_lo_ready, NB * l + k + 1)
                    for f, q in quads:
                        for u in (u_hi, u_lo)[(k == 0):]:
                            ins = pe.matmul(bank[q][:, 0:e - a], u[:, k, P * f:P * (f + 1)], counts[:, k, a:e],
                                            start=False, stop=(k == NB - 1 and u is u_lo), skip_group_check=True)
                        if k == NB - 1:
                            ins.then_inc(filled, 1)

            def turn_weights(indices):
                for i in indices:
                    pe.wait_ge(weights_summed, max(NB * r + s + 1 for r, s in TURNS[i]))
                    o = fill(("wt", i))
                    for n, (r, s) in enumerate(TURNS[i]):
                        ins = pe.transpose(o[0:BLK, BLK * n:BLK * (n + 1)], weights[:, s, BLK * r:BLK * (r + 1)],
                                           ident[0:BLK, 0:BLK])
                    ins.then_inc(filled, 1)

            for s in range(KF):
                pe.wait_ge(block_copied, NB * (NB - 1) + s + 1)
            sums(0, 0)
            fill(("cnt", 1))
            with pe.If(general > 0):
                count_sums(1, *COUNT_COLS[1], True).then_inc(filled, 1)
            with pe.Else():
                count_sums(1, *COUNT_COLS[1], False).then_inc(filled, 1)
            turn_weights((0,))
            sums(0, 1)
            for l in range(1, LAYERS):
                pe.wait_ge(*(LO_W1 if l == 1 else LO_W2))
                neighbour_terms(l, (0, 1))
                turn_weights(WT_TURNS[l])
                neighbour_terms(l, (2, 3, 4))
                own_terms(l)
                sums(l, 0)
                sums(l, 1)
                pe.wait_ge(*(LO_WF1 if l == 1 else LO_WF23))
                if l == 1:
                    head(l)
            for blocks in ((0, 1), (2,), (3,), (4,)):
                head(LAYERS - 1, blocks)
                head(LAYERS, blocks)
            pe.wait_ge(*LO_W4)
            def turn_h4(b):
                pe.wait_ge(h4_rows_ready, b + 1)
                o = fill(("h4", b))
                for f in range(KF):
                    ins = pe.transpose(o[:, BLK * f:BLK * (f + 1)], h4_rows[:, b, P * f:P * (f + 1)],
                                       ident[0:BLK, 0:BLK])
                ins.then_inc(filled, 1)

            def product_g(b):
                pe.wait_ge(h4_lo_ready, b + 1)
                project(("g", b), feature_rows(h4_hi, h4_lo, b), [(w4[0][:, k, :], w4[1][:, k, :]) for k in range(KF)])

            for b in range(3):
                turn_h4(b)
            for b in range(NB):
                product_g(b)
                if b + 3 < NB:
                    turn_h4(b + 3)
            for q, (f, h) in enumerate(AGG):
                a, e = HALVES[h]
                o = fill(("agg", q))
                for k in range(NB):
                    if q == 0:
                        pe.wait_ge(u_lo_ready, NB * LAYERS + k + 1)
                    ins = three(o[:, 0:e - a], (u_hi[:, k, P * f:P * (f + 1)], u_lo[:, k, P * f:P * (f + 1)]),
                                (weights_hi[:, k, a:e], weights_lo[:, k, a:e]), k == 0, k == NB - 1)
                ins.then_inc(filled, 1)
            for i, pairs in enumerate(Y_GROUPS):
                o = fill(("y", i))
                for n, (f, b) in enumerate(pairs):
                    pe.wait_ge(y_ready, 2 * f + (1 if b < 2 else 2))
                    ins = pe.transpose(o[0:BLK, P * n:P * (n + 1)], pre_t[:, f, BLK * b:BLK * (b + 1)], ident[:, :])
                ins.then_inc(filled, 1)


_INS = ['x', 'src', 'dst', 'edge_weight', 'L0_gnn_W0', 'L0_gnn_b0', 'L0_gnn_W1', 'L0_gnn_b1', 'L0_gnn_W2', 'L0_gnn_b2',
        'L0_gnn_Wf', 'L0_gnn_bf', 'L1_gnn_W', 'L1_gnn_bias', 'L1_gnn_gamma', 'L1_gnn_beta']


def kernel(**inputs):
    import numpy as _np
    import concourse.bacc as _bacc
    from concourse.bass_utils import run_bass_kernel_spmd as _run

    nc = _bacc.Bacc("TRN2", target_bir_lowering=False, num_devices=1)
    arrays, args = {}, []
    for name in _INS:
        a = _np.ascontiguousarray(inputs[name])
        arrays[f"in_{name}_dram"] = a
        args.append(nc.dram_tensor(f"in_{name}_dram", a.shape, mybir.dt.from_np(a.dtype), kind="ExternalInput").ap())
    args.append(nc.dram_tensor("out_dram", (NODES, D), F32, kind="ExternalOutput").ap())
    gnn_kernel(nc, *args)
    return _run(nc, [arrays], core_ids=[0]).results[0]["out_dram"]
```
